# Optimizing a Trainium2 kernel written in Bass

```python
import numpy as np
import jax
import jax.numpy as jnp

def _softmax(x, axis=-1):
    return jax.nn.softmax(x, axis=axis)

def _gelu(x):
    return jax.nn.gelu(x, approximate=True)

def _silu(x):
    return jax.nn.silu(x)

def _sigmoid(x):
    return jax.nn.sigmoid(x)

def _layernorm(x, axis=-1, eps=1e-05):
    m = jnp.mean(x, axis=axis, keepdims=True)
    v = jnp.var(x, axis=axis, keepdims=True)
    return (x - m) / jnp.sqrt(v + eps)

def _scatter_add(tgt, idx, src, axis=0):
    return tgt.at[idx].add(src)

def _segment_sum(src, seg, n):
    return jax.ops.segment_sum(src, seg, n)
kernel_name = 'mk_xattn_seq_d2_seqx_r8_51476f'

def setup_inputs(seed: int=0):
    np.random.seed(seed)
    _w = jnp.asarray

    def _rec_inputs():
        import jax
        import jax.numpy as jnp
        _rk = jax.random.key(seed)
        x = -0.0002928 + 1 * jax.random.normal(jax.random.fold_in(_rk, 1), (32, 64, 128), jnp.float32)
        _lenS = 64 - jax.random.randint(jax.random.fold_in(_rk, 7), (32,), 0, max(1, 64 // 4) + 1, jnp.int32)
        _lenS2 = 64 - jax.random.randint(jax.random.fold_in(_rk, 8), (32,), 0, max(1, 64 // 4) + 1, jnp.int32)
        _ctx_1024P = jax.random.normal(jax.random.fold_in(_rk, 11), (32, 16, 128), jnp.float32)
        _ctx_1024c = jax.random.dirichlet(jax.random.fold_in(_rk, 511), 0.3 * jnp.ones((16,), jnp.float32), (32, 64))
        _ctx_1024t = jnp.einsum('bsk,bkd->bsd', _ctx_1024c, _ctx_1024P)
        _ctx_1024t = _ctx_1024t * jax.lax.rsqrt(jnp.mean(jnp.square(_ctx_1024t)) + 1e-12) * 0.953939
        ctx_1024 = -1.39393e-06 + 0.999914 * (_ctx_1024t + 0.3 * jax.random.normal(jax.random.fold_in(_rk, 611), (32, 64, 128), jnp.float32))
        fside_Bx16xSxS2_0 = -1.47943e-05 + 1.00017 * jax.random.normal(jax.random.fold_in(_rk, 12), (32, 16, 64, 64), jnp.float32)
        return (x, ctx_1024, fside_Bx16xSxS2_0)
    x, ctx_1024, fside_Bx16xSxS2_0 = _rec_inputs()

    def _L0_xattn_setup():
        import jax, jax.numpy as jnp
        import numpy as np
        EPS = 1e-05

        def _layernorm(x, g, b):
            m = jnp.mean(x, axis=-1, keepdims=True)
            v = jnp.mean((x - m) ** 2, axis=-1, keepdims=True)
            return (x - m) / jnp.sqrt(v + EPS) * g + b

        def _mha(x, kv, Wq, Wk, Wv, mask, causal):
            m = mask[:, None]
            Q = jnp.einsum('bsd,hdk->bhsk', x, Wq) * m
            K = jnp.einsum('bsd,hdk->bhsk', kv, Wk) * m
            V = jnp.einsum('bsd,hdk->bhsk', kv, Wv) * m
            energy = jnp.einsum('bhsk,bhtk->bhst', Q, K)
            S = energy.shape[-1]
            lengths = jnp.sum(energy[:, :, 0, :] != 0, axis=-1)
            cols = jnp.arange(S)
            energy = jnp.where(cols[None, None, None, :] >= lengths[:, :, None, None], -jnp.inf, energy)
            if causal:
                energy = jnp.where(cols[None, :] > cols[:, None], -jnp.inf, energy)
            dk = Wq.shape[-1]
            score = jax.nn.softmax(energy / jnp.sqrt(jnp.asarray(dk, energy.dtype)), axis=-1)
            out = jnp.einsum('bhst,bhtk->bhsk', score, V) * m
            B, H, Sx, dkk = out.shape
            return out.transpose(0, 2, 1, 3).reshape(B, Sx, H * dkk)
        key = jax.random.key(seed)
        ks = jax.random.split(key, 20)
        B, S, D, H = (2, 256, 128, 16)
        dk = D // H
        sd = 0.02
        inp = {'x': jax.random.normal(ks[0], (B, S, D), jnp.float32), 'context': jax.random.normal(ks[1], (B, S, D), jnp.float32), 'Wq1': jax.random.normal(ks[2], (H, D, dk), jnp.float32) * sd, 'Wk1': jax.random.normal(ks[3], (H, D, dk), jnp.float32) * sd, 'Wv1': jax.random.normal(ks[4], (H, D, dk), jnp.float32) * sd, 'Wq2': jax.random.normal(ks[5], (H, D, dk), jnp.float32) * sd, 'Wk2': jax.random.normal(ks[6], (H, D, dk), jnp.float32) * sd, 'Wv2': jax.random.normal(ks[7], (H, D, dk), jnp.float32) * sd, 'ln1_g': jnp.ones((D,), jnp.float32), 'ln1_b': jnp.zeros((D,), jnp.float32), 'ln2_g': jnp.ones((D,), jnp.float32), 'ln2_b': jnp.zeros((D,), jnp.float32), 'ln3_g': jnp.ones((D,), jnp.float32), 'ln3_b': jnp.zeros((D,), jnp.float32), 'fc1_w': jax.random.normal(ks[8], (D, D), jnp.float32) * sd, 'fc1_b': jnp.zeros((D,), jnp.float32), 'fc2_w': jax.random.normal(ks[9], (D, D), jnp.float32) * sd, 'fc2_b': jnp.zeros((D,), jnp.float32)}
        return inp
    _L0_xattn_all = _L0_xattn_setup()
    _L0_xattn_in = {k: v for k, v in _L0_xattn_all.items() if k in ('Wq1', 'Wk1', 'Wv1', 'Wq2', 'Wk2', 'Wv2', 'ln1_g', 'ln1_b', 'ln2_g', 'ln2_b', 'ln3_g', 'ln3_b', 'fc1_w', 'fc1_b', 'fc2_w', 'fc2_b')}
    del _L0_xattn_all

    def _L1_xattn_setup():
        import jax, jax.numpy as jnp
        import numpy as np
        N_HEADS = 16
        D_MODEL = 128
        D_K = 64
        D_V = 64
        LN_EPS = 1e-06
        key = jax.random.key(seed)
        ks = jax.random.split(key, 16)
        B, L, D = (4, 64, D_MODEL)
        s = 1.0 / np.sqrt(D)
        return {'q': jax.random.normal(ks[0], (B, L, D), jnp.float32), 'k': jax.random.normal(ks[1], (B, L, D), jnp.float32), 'v': jax.random.normal(ks[2], (B, L, D), jnp.float32), 'bias': jax.random.normal(ks[3], (B, N_HEADS, L, L), jnp.float32), 'graph_attn_bias': jax.random.normal(ks[4], (B, N_HEADS, L, L), jnp.float32), 'wq': jax.random.normal(ks[5], (D, N_HEADS * D_K), jnp.float32) * s, 'bq': jnp.zeros((N_HEADS * D_K,), jnp.float32), 'wk': jax.random.normal(ks[6], (D, N_HEADS * D_K), jnp.float32) * s, 'bk': jnp.zeros((N_HEADS * D_K,), jnp.float32), 'wv': jax.random.normal(ks[7], (D, N_HEADS * D_V), jnp.float32) * s, 'bv': jnp.zeros((N_HEADS * D_V,), jnp.float32), 'wo': jax.random.normal(ks[8], (N_HEADS * D_V, D), jnp.float32) * s, 'bo': jnp.zeros((D,), jnp.float32), 'ln_g': jnp.ones((D,), jnp.float32), 'ln_b': jnp.zeros((D,), jnp.float32)}
    _L1_xattn_all = _L1_xattn_setup()
    _L1_xattn_in = {k: v for k, v in _L1_xattn_all.items() if k in ('wq', 'bq', 'wk', 'bk', 'wv', 'bv', 'wo', 'bo', 'ln_g', 'ln_b')}
    del _L1_xattn_all
    return {'x': x, 'ctx_1024': ctx_1024, 'fside_Bx16xSxS2_0': fside_Bx16xSxS2_0, 'L0_xattn_Wq1': _L0_xattn_in['Wq1'], 'L0_xattn_Wk1': _L0_xattn_in['Wk1'], 'L0_xattn_Wv1': _L0_xattn_in['Wv1'], 'L0_xattn_Wq2': _L0_xattn_in['Wq2'], 'L0_xattn_Wk2': _L0_xattn_in['Wk2'], 'L0_xattn_Wv2': _L0_xattn_in['Wv2'], 'L0_xattn_ln1_g': _L0_xattn_in['ln1_g'], 'L0_xattn_ln1_b': _L0_xattn_in['ln1_b'], 'L0_xattn_ln2_g': _L0_xattn_in['ln2_g'], 'L0_xattn_ln2_b': _L0_xattn_in['ln2_b'], 'L0_xattn_ln3_g': _L0_xattn_in['ln3_g'], 'L0_xattn_ln3_b': _L0_xattn_in['ln3_b'], 'L0_xattn_fc1_w': _L0_xattn_in['fc1_w'], 'L0_xattn_fc1_b': _L0_xattn_in['fc1_b'], 'L0_xattn_fc2_w': _L0_xattn_in['fc2_w'], 'L0_xattn_fc2_b': _L0_xattn_in['fc2_b'], 'L1_xattn_wq': _L1_xattn_in['wq'], 'L1_xattn_bq': _L1_xattn_in['bq'], 'L1_xattn_wk': _L1_xattn_in['wk'], 'L1_xattn_bk': _L1_xattn_in['bk'], 'L1_xattn_wv': _L1_xattn_in['wv'], 'L1_xattn_bv': _L1_xattn_in['bv'], 'L1_xattn_wo': _L1_xattn_in['wo'], 'L1_xattn_bo': _L1_xattn_in['bo'], 'L1_xattn_ln_g': _L1_xattn_in['ln_g'], 'L1_xattn_ln_b': _L1_xattn_in['ln_b']}

def reference(x, ctx_1024, fside_Bx16xSxS2_0, L0_xattn_Wq1, L0_xattn_Wk1, L0_xattn_Wv1, L0_xattn_Wq2, L0_xattn_Wk2, L0_xattn_Wv2, L0_xattn_ln1_g, L0_xattn_ln1_b, L0_xattn_ln2_g, L0_xattn_ln2_b, L0_xattn_ln3_g, L0_xattn_ln3_b, L0_xattn_fc1_w, L0_xattn_fc1_b, L0_xattn_fc2_w, L0_xattn_fc2_b, L1_xattn_wq, L1_xattn_bq, L1_xattn_wk, L1_xattn_bk, L1_xattn_wv, L1_xattn_bv, L1_xattn_wo, L1_xattn_bo, L1_xattn_ln_g, L1_xattn_ln_b):
    import jax
    import jax.numpy as jnp

    def _L0_xattn_ref(x, context, Wq1, Wk1, Wv1, Wq2, Wk2, Wv2, ln1_g, ln1_b, ln2_g, ln2_b, ln3_g, ln3_b, fc1_w, fc1_b, fc2_w, fc2_b):
        import jax, jax.numpy as jnp
        import numpy as np
        EPS = 1e-05

        def _layernorm(x, g, b):
            m = jnp.mean(x, axis=-1, keepdims=True)
            v = jnp.mean((x - m) ** 2, axis=-1, keepdims=True)
            return (x - m) / jnp.sqrt(v + EPS) * g + b

        def _mha(x, kv, Wq, Wk, Wv, mask, causal):
            m = mask[:, None]
            Q = jnp.einsum('bsd,hdk->bhsk', x, Wq) * m
            K = jnp.einsum('bsd,hdk->bhsk', kv, Wk) * m
            V = jnp.einsum('bsd,hdk->bhsk', kv, Wv) * m
            energy = jnp.einsum('bhsk,bhtk->bhst', Q, K)
            S = energy.shape[-1]
            lengths = jnp.sum(energy[:, :, 0, :] != 0, axis=-1)
            cols = jnp.arange(S)
            energy = jnp.where(cols[None, None, None, :] >= lengths[:, :, None, None], -jnp.inf, energy)
            if causal:
                energy = jnp.where(cols[None, :] > cols[:, None], -jnp.inf, energy)
            dk = Wq.shape[-1]
            score = jax.nn.softmax(energy / jnp.sqrt(jnp.asarray(dk, energy.dtype)), axis=-1)
            out = jnp.einsum('bhst,bhtk->bhsk', score, V) * m
            B, H, Sx, dkk = out.shape
            return out.transpose(0, 2, 1, 3).reshape(B, Sx, H * dkk)
        mask0 = 1.0 - jnp.all(x == 0, axis=2, keepdims=True).astype(x.dtype)
        z = _mha(x, x, Wq1, Wk1, Wv1, mask0, causal=True)
        x1 = _layernorm(x + z, ln1_g, ln1_b)
        mask1 = 1.0 - jnp.all(x1 == 0, axis=2, keepdims=True).astype(x1.dtype)
        z = _mha(x1, context, Wq2, Wk2, Wv2, mask1, causal=False)
        x2 = _layernorm(x1 + z, ln2_g, ln2_b)
        z = jnp.maximum(x2 @ fc1_w.T + fc1_b, 0.0) * mask0
        z = (z @ fc2_w.T + fc2_b) * mask0
        return _layernorm(x2 + z, ln3_g, ln3_b)

    def _L1_xattn_ref(q, k, v, bias, graph_attn_bias, wq, bq, wk, bk, wv, bv, wo, bo, ln_g, ln_b):
        import jax, jax.numpy as jnp
        import numpy as np
        N_HEADS = 16
        D_MODEL = 128
        D_K = 64
        D_V = 64
        LN_EPS = 1e-06
        B, Lq, D = q.shape
        H, dk, dv = (N_HEADS, D_K, D_V)
        residual = q
        qh = (q @ wq + bq).reshape(B, Lq, H, dk).transpose(0, 2, 1, 3)
        kh = (k @ wk + bk).reshape(B, k.shape[1], H, dk).transpose(0, 2, 1, 3)
        vh = (v @ wv + bv).reshape(B, v.shape[1], H, dv).transpose(0, 2, 1, 3)
        scores = jnp.einsum('bhqd,bhkd->bhqk', qh / np.sqrt(dk).astype(qh.dtype), kh)
        scores = scores + bias + graph_attn_bias
        weights = jax.nn.softmax(scores, axis=-1)
        ctx = jnp.einsum('bhqk,bhkd->bhqd', weights, vh)
        ctx = ctx.transpose(0, 2, 1, 3).reshape(B, Lq, H * dv)
        out = ctx @ wo + bo + residual
        mu = jnp.mean(out, axis=-1, keepdims=True)
        var = jnp.var(out, axis=-1, keepdims=True)
        out = (out - mu) * jax.lax.rsqrt(var + LN_EPS) * ln_g + ln_b
        return out
    x = _L0_xattn_ref(x, ctx_1024, L0_xattn_Wq1, L0_xattn_Wk1, L0_xattn_Wv1, L0_xattn_Wq2, L0_xattn_Wk2, L0_xattn_Wv2, L0_xattn_ln1_g, L0_xattn_ln1_b, L0_xattn_ln2_g, L0_xattn_ln2_b, L0_xattn_ln3_g, L0_xattn_ln3_b, L0_xattn_fc1_w, L0_xattn_fc1_b, L0_xattn_fc2_w, L0_xattn_fc2_b)
    x = _L1_xattn_ref(x, ctx_1024, ctx_1024, fside_Bx16xSxS2_0, fside_Bx16xSxS2_0, L1_xattn_wq, L1_xattn_bq, L1_xattn_wk, L1_xattn_bk, L1_xattn_wv, L1_xattn_bv, L1_xattn_wo, L1_xattn_bo, L1_xattn_ln_g, L1_xattn_ln_b)
    return x

_drawn_inputs = setup_inputs


def setup_inputs(seed=0):
    import zlib

    import numpy as np

    out = dict(_drawn_inputs(seed))
    spreads = {'L0_xattn_ln1_g': (1.0, 0.2),
     'L0_xattn_ln1_b': (0.0, 0.1),
     'L0_xattn_ln2_g': (1.0, 0.2),
     'L0_xattn_ln2_b': (0.0, 0.1),
     'L0_xattn_ln3_g': (1.0, 0.2),
     'L0_xattn_ln3_b': (0.0, 0.1),
     'L0_xattn_fc1_b': (0.0, 0.8),
     'L0_xattn_fc2_b': (0.0, 0.1),
     'L1_xattn_bq': (0.0, 0.1),
     'L1_xattn_bk': (0.0, 0.8),
     'L1_xattn_bv': (0.0, 0.1),
     'L1_xattn_bo': (0.0, 0.1),
     'L1_xattn_ln_g': (1.0, 0.2),
     'L1_xattn_ln_b': (0.0, 0.1)}
    factors = {'L0_xattn_Wq1': 8.0,
     'L0_xattn_Wk1': 8.0,
     'L0_xattn_Wq2': 8.0,
     'L0_xattn_Wk2': 8.0,
     'L0_xattn_fc1_w': 3.009}
    for name, (base, spread) in spreads.items():
        noise = np.random.default_rng([zlib.crc32(name.encode()), seed]).standard_normal(out[name].shape)
        drawn = base * np.exp(spread * noise) if base else spread * noise
        out[name] = jnp.asarray(drawn.astype(out[name].dtype))
    for name, factor in factors.items():
        out[name] = (out[name] * factor).astype(out[name].dtype)
    return out
```

```python
from contextlib import ExitStack

import numpy as np

import concourse.bass as bass
from concourse import mybir

F32 = mybir.dt.float32
BF16 = mybir.dt.bfloat16
ALU = mybir.AluOpType
ACT = mybir.ActivationFunctionType
AX = mybir.AxisListType

P = 128
B, S, D, H = 32, 64, 128, 16
PAIRS = B // 2
DK0 = D // H
DK1 = 64
HD = H * DK1
J = H // 2
HALF = 512
EPS0, EPS1 = 1e-5, 1e-6
BIG = -1e30
SLOT = 16

CONST = dict(ident=P, blockones=P, hmask=H, vmask=P, iota=S * H, row1=1, power=1, eps0=1, eps1=1)


def constants():
    p = np.arange(P)
    c = {
        "ident": np.eye(P),
        "blockones": p[:, None] // S == p[None] // S,
        "hmask": p[:, None] // DK0 == np.arange(H)[None],
        "vmask": p[:, None] // S == (np.arange(P)[None] // DK0) % 2,
        "iota": np.broadcast_to(np.repeat(np.arange(S), H)[None], (P, S * H)),
        "row1": p[:, None] % S + 1,
        "power": np.full((P, 1), -0.5),
        "eps0": np.full((P, 1), EPS0),
        "eps1": np.full((P, 1), EPS1),
    }
    return np.concatenate([c[k].astype(np.float32) for k in CONST], axis=1)


ATT = ["qkv", "qk", "q0", "kblk", "v", "e0", "nz", "cnt", "thr", "e_0", "max_0", "exp_0", "e_1", "max_1",
       "pt_0", "exp_1", "pts_0", "pt_1", "pts_1", "pv", "zts", "z", "zn", "ln1", "ln2", "ln3"]


def bass_two_blocks(nc, consts, x, xT, ctxn, ctxT, fs, Wq1, Wk1, Wv1, Wq2, Wk2, Wv2, fc1T, fc2T,
                    vecs, fc1b, wq, wk, wv, wo, bq, bk, bv, out):
    with ExitStack() as stack:
        def sb(name, shape, dt=F32):
            return stack.enter_context(nc.sbuf_tensor(name, shape, dt))

        def ps(name):
            return stack.enter_context(nc.psum_tensor(name, [P, HALF], F32))

        def sem(name):
            return stack.enter_context(nc.semaphore(name))

        cst = sb("cst", [P, sum(CONST.values())])
        at, cut = {}, 0
        for k, w in CONST.items():
            at[k] = cst[:, cut:cut + w]
            cut += w
        ident = at["ident"]
        bones = sb("bones", [P, P], BF16)
        bigid = sb("bigid", [P, P], BF16)
        iota = sb("iota", [P, S, H], BF16)
        W = {}
        for n in ("Wq1", "Wk1", "Wv1", "Wq2", "Wk2", "Wv2", "fc1T", "fc2T"):
            W[n] = sb(n + "_sb", [P, P])
        wq_sb, wk_sb, wv_sb = (sb(n, [P, HD]) for n in ("wq_sb", "wk_sb", "wv_sb"))
        wo_sb = sb("wo_sb", [P, J, D])
        VEC = ("ln1_g", "ln1_b", "ln2_g", "ln2_b", "ln3_g", "ln3_b", "ln_g", "ln_b", "bo", "fc2_b")
        vec_sb = sb("vec_sb", [P, len(VEC), D])
        vec = {n: vec_sb[:, k, :] for k, n in enumerate(VEC)}
        fc1b_sb = sb("fc1b_sb", [P, 1])
        bq_sb, bk_sb, bv_sb = (sb(n, [P, J]) for n in ("bq_sb", "bk_sb", "bv_sb"))
        bq8 = sb("bq8", [P, J])
        obias = sb("obias", [P, D])
        w_self, w_block0, w_block1 = sem("w_self"), sem("w_block0"), sem("w_block1")
        ready, zeroed = sem("ready"), sem("zeroed")
        bvo_ready = sem("bvo_ready")

        class Ns:
            pass

        def attention(name):
            a = Ns()
            a.E, a.X = ps(name + "_E"), ps(name + "_X")
            a.qk = sb(name + "_qk", [P, 2, P])
            a.kblk = sb(name + "_kblk", [P, H, P])
            a.q0 = sb(name + "_q0", [P, 2, H])
            a.nz = sb(name + "_nz", [P, H], BF16)
            a.thr = sb(name + "_thr", [P, H], BF16)
            a.lenpos = sb(name + "_lenpos", [P, H])
            a.mask = sb(name + "_mask", [P, S, H], BF16)
            a.mx = sb(name + "_mx", [P, H])
            a.S = sb(name + "_S", [P, H * S])
            a.V = sb(name + "_V", [P, 2, H, SLOT])
            a.PT = sb(name + "_PT", [P, H * S])
            a.zT = sb(name + "_zT", [P, 2, P])
            a.den = sb(name + "_den", [P, H])
            a.rd = sb(name + "_rd", [P, H])
            a.zn = sb(name + "_zn", [P, D])
            a.s_qkv = sem(name + "_qkv")
            a.s_qk = sem(name + "_qk")
            a.s_q0 = sem(name + "_q0")
            a.s_v = sem(name + "_v")
            a.s_kblk = sem(name + "_kblk")
            a.s_e0 = sem(name + "_e0")
            a.s_nz = sem(name + "_nz")
            a.s_cnt = sem(name + "_cnt")
            a.s_thr = sem(name + "_thr")
            a.s_mask = sem(name + "_mask")
            a.s_e = sem(name + "_e")
            a.s_max = sem(name + "_max")
            a.s_sub = sem(name + "_sub")
            a.s_p = sem(name + "_p")
            a.s_pt = sem(name + "_pt")
            a.s_pts = sem(name + "_pts")
            a.s_zt = sem(name + "_zt")
            a.s_zts = sem(name + "_zts")
            a.s_z = sem(name + "_z")
            a.s_zn = sem(name + "_zn")
            return a

        def norm(name, g, b, eps, out_ap):
            l = Ns()
            l.y = sb(name + "_y", [P, D])
            l.st = sb(name + "_st", [P, 6])
            l.mv = sb(name + "_mv", [P, 2])
            l.ve = sb(name + "_ve", [P, 1])
            l.rstd = sb(name + "_rstd", [P, 1])
            l.xh = sb(name + "_xh", [P, D])
            l.xg = sb(name + "_xg", [P, D])
            l.g, l.b, l.eps, l.out = vec[g], vec[b], eps, out_ap
            l.s_y, l.s_st, l.s_rstd, l.s_xh, l.s_xg, l.s_out = (
                sem(name + "_" + s) for s in ("y", "st", "rstd", "xh", "xg", "out"))
            return l

        h1 = sb("h1", [P, D + 1])
        h2 = sb("h2", [P, D])
        x2 = sb("x2", [P, D])
        osb = sb("osb", [P, D])
        A, Bc = attention("A"), attention("B")
        L1 = norm("L1", "ln1_g", "ln1_b", "eps0", h1[:, 0:D])
        L2 = norm("L2", "ln2_g", "ln2_b", "eps0", x2[:])
        L3 = norm("L3", "ln3_g", "ln3_b", "eps0", h2[:])
        L4 = norm("L4", "ln_g", "ln_b", "eps1", osb[:])

        A.xT, A.xn, A.am = sb("A_xT", [P, P]), sb("A_xn", [P, D]), sb("A_am", [P, 1])
        s_xTl, s_xnl, s_m0 = sem("s_xTl"), sem("s_xnl"), sem("s_m0")
        x1r = sb("x1r", [P, D + 1])
        cn, cm, xc = sb("cn", [P, D]), sb("cm", [P, D]), sb("xc", [P, 2, P])
        am1, m1 = sb("am1", [P, 1]), sb("m1", [P, 1])
        x2T, hT, ffn = sb("x2T", [P, P]), sb("hT", [P, P]), sb("ffn", [P, D])
        s_cnl, s_h1c, s_cm, s_xt, s_xts = (sem(n) for n in ("s_cnl", "s_h1c", "s_cm", "s_xt", "s_xts"))
        s_f1, s_f1s, s_f2, s_f2s, s_f3, s_ffn = (sem(n) for n in ("s_f1", "s_f1s", "s_f2", "s_f2s", "s_f3", "s_ffn"))
        C = Ns()
        C.E, C.X = [ps("C_E0"), ps("C_E1")], [ps("C_X0"), ps("C_X1")]
        cT, f = sb("cT", [P, P]), sb("f", [P, H, S])
        kst, Kz = sb("kst", [P, J, P]), sb("Kz", [P, 2, J, P])
        vst, Vz = sb("vst", [P, 2, HALF]), sb("Vz", [P, 2, 2, HALF])
        x3T, x3r, qT = sb("x3T", [P, P]), sb("x3r", [P, D]), sb("qT", [P, J, P])
        Sc, Pc = sb("Sc", [P, H * S]), sb("Pc", [P, H * S])
        mxc, denc, rdc = sb("mxc", [P, H]), sb("denc", [P, H]), sb("rdc", [P, H])
        PTc, ctxs, ctxTs = sb("PTc", [P, H * S]), sb("ctxs", [P, HD]), sb("ctxTs", [P, J, P])
        C.s_cTl = sem("C_cTl")
        C.s_fl = sem("C_fl")
        C.s_k = sem("C_k")
        C.s_ks = sem("C_ks")
        C.s_kz = sem("C_kz")
        C.s_v = sem("C_v")
        C.s_vs = sem("C_vs")
        C.s_vz = sem("C_vz")
        C.s_x3t = sem("C_x3t")
        C.s_x3ts = sem("C_x3ts")
        C.s_x3r = sem("C_x3r")
        C.s_q = sem("C_q")
        C.s_qs = sem("C_qs")
        C.s_e = sem("C_e")
        C.s_s = sem("C_s")
        C.s_max = sem("C_max")
        C.s_sub = sem("C_sub")
        C.s_p = sem("C_p")
        C.s_den = sem("C_den")
        C.s_rd = sem("C_rd")
        C.s_pt = sem("C_pt")
        C.s_pts = sem("C_pts")
        C.s_ctx = sem("C_ctx")
        C.s_cn = sem("C_cn")
        C.s_ct = sem("C_ct")
        C.s_cts = sem("C_cts")
        C.s_o = sem("C_o")
        s_st = sem("s_stored")
        passed = sem("passed")

        def reused(n):
            return not isinstance(n, int) or n > 0

        def heads(ap):
            return ap.rearrange("p (h t) -> p h t", t=S)

        def run(eng, steps, body_counts):
            first, last = body_counts

            def body(i):
                for chain, step, ahead in ORDER:
                    fn = steps.get(chain + "." + step)
                    n = i + ahead
                    if fn and not (isinstance(n, int) and not 0 <= n < PAIRS):
                        fn(n)

            for i in range(-AHEAD, first):
                body(i)
            with eng.Fori(first, last) as i:
                body(i)
            for i in range(last, PAIRS):
                body(i)

        ENG = (1, PAIRS - AHEAD)
        SPR = (1, PAIRS - AHEAD - 1)

        block = stack.enter_context(nc.Block())

        @block.sync
        def _(sp):
            sp.dma_start(cst[:], consts).then_inc(w_self, 16)
            for n, ap in (("Wq1", Wq1), ("Wk1", Wk1), ("Wv1", Wv1)):
                sp.dma_start(W[n][:], ap).then_inc(w_self, 16)

            def pair(ap, n):
                return ap[bass.ds(n * P, P), :]

            def load_x(n):
                if reused(n):
                    sp.wait_ge(A.s_qkv, n)
                sp.dma_start(A.xT[:], xT[:, bass.ds(n * P, P)]).then_inc(s_xTl, 16)
                if reused(n):
                    sp.wait_ge(L1.s_y, n)
                sp.dma_start(A.xn[:], pair(x, n)).then_inc(s_xnl, 16)

            def load_cn(n):
                if reused(n):
                    sp.wait_ge(s_cm, 3 * n)
                sp.dma_start(cn[:], pair(ctxn, n)).then_inc(s_cnl, 16)

            def load_c(n):
                if reused(n):
                    sp.wait_ge(C.s_v, 2 * n)
                sp.dma_start(cT[:], ctxT[:, bass.ds(n * P, P)]).then_inc(C.s_cTl, 16)

            def load_f(n):
                if reused(n):
                    sp.wait_ge(C.s_s, 2 * n)
                sp.dma_start(f[:].rearrange("p h t -> p (h t)"), pair(fs, n)).then_inc(C.s_fl, 16)

            load_x(0)
            for n, ap in (("Wq2", Wq2), ("Wk2", Wk2), ("Wv2", Wv2), ("fc1T", fc1T), ("fc2T", fc2T)):
                sp.dma_start(W[n][:], ap).then_inc(w_block0, 16)
            sp.dma_start(vec_sb[:], vecs.rearrange("(o v) d -> o v d", o=1).to_broadcast([P, len(VEC), D])
                         ).then_inc(w_block0, 16)
            sp.dma_start(fc1b_sb[:], fc1b).then_inc(w_block0, 16)
            load_cn(0)
            for t, ap in ((bq_sb, bq), (bk_sb, bk), (bv_sb, bv)):
                sp.dma_start(t[:], ap).then_inc(w_block0, 16)
            for t, ap in ((wk_sb, wk), (wv_sb, wv), (wq_sb, wq)):
                sp.dma_start(t[:], ap).then_inc(w_block1, 16)
            sp.dma_start(wo_sb[:], wo.rearrange("(j p) d -> p j d", p=P)).then_inc(w_block1, 16)
            load_c(0)
            load_f(0)

            def next_pair(load):
                def step(n):
                    if isinstance(n, int) and n + 1 >= PAIRS:
                        return
                    load(n + 1)
                return step

            def kz(n):
                sp.wait_ge(C.s_ks, 2 * n + 2)
                if reused(n):
                    sp.wait_ge(C.s_e, 2 * n)
                if isinstance(n, int) and n == 0:
                    sp.wait_ge(zeroed, 2)
                for hl in range(2):
                    r = slice(64 * hl, 64 * hl + 64)
                    sp.dma_start(Kz[r, hl], kst[r]).then_inc(C.s_kz, 16)

            def vz(n):
                sp.wait_ge(C.s_vs, 2 * n + 2)
                if reused(n):
                    sp.wait_ge(C.s_ctx, 2 * n)
                for hl in range(2):
                    r = slice(64 * hl, 64 * hl + 64)
                    sp.dma_start(Vz[r, :, hl], vst[r]).then_inc(C.s_vz, 16)

            def store(n):
                sp.wait_ge(L4.s_out, n + 1)
                sp.dma_start(pair(out, n), osb[:]).then_inc(s_st, 16)

            run(sp, {"A.y": next_pair(load_x), "B.cm": next_pair(load_cn), "C.v": next_pair(load_c),
                     "C.fadd_1": next_pair(load_f), "C.kz": kz, "C.vz": vz, "C.store": store}, SPR)
            sp.wait_ge(s_st, 16 * PAIRS)

        @block.tensor
        def _(pe):
            mm, tr = nc.tensor.matmul, nc.tensor.transpose

            def qkv(a, wqkv, xq, xkv):
                def step(n):
                    if a is A:
                        pe.wait_ge(s_xTl, 16 * n + 16)
                        if reused(n):
                            pe.wait_ge(A.s_zn, 3 * n)
                    else:
                        pe.wait_ge(s_xts, n + 1)
                    mm(a.X[:, 0:P], wqkv[0][:], xq, start=True, stop=True)
                    mm(a.X[:, P:2 * P], wqkv[1][:], xkv, start=True, stop=True)
                    for b in range(2):
                        for r in range(2):
                            last = mm(a.X[S * r:S * r + S, (2 + b) * P:(3 + b) * P], xkv[:, S * b:S * b + S],
                                      wqkv[2][:], start=True, stop=True)
                    last.then_inc(a.s_qkv, 1)
                return step

            def e0(a):
                def step(n):
                    pe.wait_ge(a.s_q0, 2 * n + 2)
                    if reused(n):
                        pe.wait_ge(a.s_zts, n)
                    for b in range(2):
                        last = mm(a.E[S * b:S * b + S, 0:H], a.qk[:, 1, S * b:S * b + S], a.q0[:, b], start=True,
                                  stop=True)
                    last.then_inc(a.s_e0, 1)
                return step

            def cnt(a):
                def step(n):
                    pe.wait_ge(a.s_nz, n + 1)
                    mm(a.E[:, H:2 * H], bones[:], a.nz[:], start=True, stop=True).then_inc(a.s_cnt, 1)
                return step

            def energy(a, hf):
                def step(n):
                    pe.wait_ge(a.s_kblk, 2 * n + 1 + hf)
                    if hf == 0:
                        pe.wait_ge(a.s_thr, 2 * n + 2)
                    else:
                        pe.wait_ge(a.s_sub, 2 * n + 1)
                    for b in range(2):
                        mm(a.E[S * b:S * b + S, :], a.qk[:, 0, S * b:S * b + S],
                           a.kblk[:, 8 * hf:8 * hf + 8, S * b:S * b + S], start=True, stop=False,
                           skip_group_check=True)
                    pe.wait_ge(a.s_mask, n + 1)
                    mm(a.E[:, :], bigid[:], a.mask[:, :, 8 * hf:8 * hf + 8].rearrange("p t h -> p h t"),
                       start=False, stop=True, skip_group_check=True).then_inc(a.s_e, 1)
                return step

            def pt(a, hf):
                def step(n):
                    pe.wait_ge(a.s_p, 2 * n + 1 + hf)
                    if hf == 0:
                        pe.wait_ge(a.s_v, 2 * n + 2)
                    else:
                        pe.wait_ge(a.s_pts, 2 * n + 1)
                    for j in range(4):
                        last = tr(a.X[:, j * P:(j + 1) * P], a.S[:, (4 * hf + j) * P:(4 * hf + j + 1) * P], ident)
                    last.then_inc(a.s_pt, 1)
                return step

            def pv(a):
                def step(n):
                    pe.wait_ge(a.s_pts, 2 * n + 2)
                    pe.wait_ge(a.s_sub, 2 * n + 2)
                    for j in range(J):
                        for b in range(2):
                            q = 32 * (j % 4)
                            c = (j // 4) * P + S * b
                            last = mm(a.E[q:q + 32, c:c + S], a.V[:, b, 2 * j:2 * j + 2].rearrange("p a c -> p (a c)"),
                                      a.PT[:, j * P + S * b:j * P + S * b + S], start=True, stop=True)
                    last.then_inc(a.s_zt, 1)
                return step

            def z(a):
                def step(n):
                    pe.wait_ge(a.s_zts, n + 1)
                    for c in range(2):
                        last = tr(a.X[:, c * P:(c + 1) * P], a.zT[:, c], ident)
                    last.then_inc(a.s_z, 1)
                return step

            def b_tr(n):
                pe.wait_ge(s_cm, 3 * n + 3)
                if reused(n):
                    pe.wait_ge(s_ffn, n)
                tr(Bc.X[:, 0:P], x1r[:, 0:D], ident)
                tr(Bc.X[:, P:2 * P], cm[:], ident).then_inc(s_xt, 1)

            def f1(n):
                pe.wait_ge(L2.s_out, n + 1)
                tr(Bc.X[:, 0:P], x2[:], ident).then_inc(s_f1, 1)

            def f2(n):
                pe.wait_ge(s_f1s, n + 1)
                mm(Bc.E[:, 0:P], W["fc1T"][:], x2T[:], start=True, stop=True).then_inc(s_f2, 1)

            def f3(n):
                pe.wait_ge(s_f2s, n + 1)
                mm(Bc.X[:, 0:P], hT[:], W["fc2T"][:], start=True, stop=True).then_inc(s_f3, 1)

            def c_k(n):
                pe.wait_ge(C.s_cTl, 16 * n + 16)
                if isinstance(n, int) and n == 0:
                    pe.wait_ge(w_block1, 16 * 4)
                    for j in range(J):
                        last = mm(C.E[0][:, 0:D], bv_sb[:, j:j + 1].to_broadcast([P, P]), wo_sb[:, j], start=(j == 0),
                                  stop=(j == J - 1))
                    last.then_inc(bvo_ready, 1)
                for g in range(2):
                    if reused(n):
                        pe.wait_ge(C.s_cts, 2 * n)
                    for j in range(4):
                        c = (4 * g + j) * P
                        last = mm(C.X[g][:, j * P:(j + 1) * P], wk_sb[:, c:c + P], cT[:], start=True, stop=True)
                    last.then_inc(C.s_k, 1)

            def c_v(n):
                wv_v = wv_sb[:].rearrange("p (j l d) -> p l j d", l=2, d=DK1)
                for b in range(2):
                    pe.wait_ge(C.s_ks, 2 * n + 1 + b)
                    for hl in range(2):
                        last = mm(C.X[b][S * hl:S * hl + S, :], cT[:, S * b:S * b + S], wv_v[:, hl], start=True,
                                  stop=True)
                    last.then_inc(C.s_v, 1)

            def c_x3t(n):
                pe.wait_ge(L3.s_out, n + 1)
                pe.wait_ge(C.s_vs, 2 * n + 1)
                tr(C.X[0][:, 0:P], h2[:], ident).then_inc(C.s_x3t, 1)

            def c_q(n):
                pe.wait_ge(C.s_x3ts, n + 1)
                pe.wait_ge(C.s_vs, 2 * n + 2)
                for g in range(2):
                    for j in range(4):
                        c = (4 * g + j) * P
                        last = mm(C.X[g][:, j * P:(j + 1) * P], wq_sb[:, c:c + P], x3T[:], start=True, stop=True)
                    last.then_inc(C.s_q, 1)

            def c_e(g):
                def step(n):
                    pe.wait_ge(C.s_qs, 2 * n + 1 + g)
                    if g == 0:
                        pe.wait_ge(C.s_kz, 32 * n + 32)
                        if reused(n):
                            pe.wait_ge(L4.s_y, n)
                    if isinstance(n, int) and n == 0:
                        pe.wait_ge(bvo_ready, 2)
                    for j in range(4):
                        for b in range(2):
                            last = mm(C.E[g][S * b:S * b + S, j * P:(j + 1) * P], qT[:, 4 * g + j, S * b:S * b + S],
                                      Kz[:, :, 4 * g + j, S * b:S * b + S], start=True, stop=True)
                    last.then_inc(C.s_e, 1)
                return step

            def c_pt(g):
                def step(n):
                    pe.wait_ge(C.s_p, 2 * n + 1 + g)
                    pe.wait_ge(C.s_qs, 2 * n + 1 + g)
                    for j in range(4):
                        c = (4 * g + j) * P
                        last = tr(C.X[g][:, j * P:(j + 1) * P], Pc[:, c:c + P], ident)
                    last.then_inc(C.s_pt, 1)
                return step

            def c_ctx(g):
                def step(n):
                    pe.wait_ge(C.s_pts, 2 * n + 1 + g)
                    pe.wait_ge(C.s_vz, 32 * n + 32)
                    pe.wait_ge(C.s_s, 2 * n + 1 + g)
                    for j in range(4):
                        for b in range(2):
                            c = (4 * g + j) * P + S * b
                            vz = Vz[:, b, :, (4 * g + j) * DK1:(4 * g + j + 1) * DK1]
                            last = mm(C.E[g][S * b:S * b + S, j * P:(j + 1) * P], PTc[:, c:c + S], vz, start=True,
                                      stop=True)
                    last.then_inc(C.s_ctx, 1)
                return step

            def c_ct(g):
                def step(n):
                    pe.wait_ge(C.s_cn, 2 * n + 1 + g)
                    pe.wait_ge(C.s_pts, 2 * n + 1 + g)
                    for j in range(4):
                        c = (4 * g + j) * P
                        last = tr(C.X[g][:, j * P:(j + 1) * P], ctxs[:, c:c + P], ident)
                    last.then_inc(C.s_ct, 1)
                return step

            def c_o(n):
                pe.wait_ge(C.s_cts, 2 * n + 2)
                for j in range(J):
                    last = mm(C.E[0][:, 0:D], ctxTs[:, j], wo_sb[:, j], start=(j == 0), stop=(j == J - 1))
                last.then_inc(C.s_o, 1)

            steps = {"B.tr": b_tr, "B.f1": f1, "B.f2": f2, "B.f3": f3, "C.k": c_k, "C.v": c_v, "C.x3t": c_x3t,
                     "C.q": c_q, "C.o": c_o,
                     "A.qkv": qkv(A, [W[n] for n in ("Wq1", "Wk1", "Wv1")], A.xT[:], A.xT[:]),
                     "B.qkv": qkv(Bc, [W[n] for n in ("Wq2", "Wk2", "Wv2")], xc[:, 0], xc[:, 1])}
            for g in range(2):
                steps |= {f"C.e_{g}": c_e(g), f"C.pt_{g}": c_pt(g), f"C.ctx_{g}": c_ctx(g), f"C.ct_{g}": c_ct(g)}
            for nm, a in (("A", A), ("B", Bc)):
                steps |= {nm + ".e0": e0(a), nm + ".cnt": cnt(a), nm + ".e_0": energy(a, 0), nm + ".e_1": energy(a, 1),
                          nm + ".pt_0": pt(a, 0), nm + ".pt_1": pt(a, 1), nm + ".pv": pv(a), nm + ".z": z(a)}
            pe.wait_ge(w_self, 16 * 4)
            pe.wait_ge(w_block0, 16 * 10)
            pe.wait_ge(ready, 7)
            run(pe, steps, ENG)

        @block.scalar
        def _(act):
            def qk(a):
                def step(n):
                    act.wait_ge(a.s_qkv, n + 1)
                    act.copy(a.qk[:].rearrange("p a c -> p (a c)"), a.X[:, 0:2 * P]).then_inc(a.s_qk, 1)
                return step

            def exp(a, hf):
                def step(n):
                    act.wait_ge(a.s_sub, 2 * n + 1 + hf)
                    v = a.S[:, hf * HALF:(hf + 1) * HALF]
                    act.activation(v, v, ACT.Exp, scale=float(DK0) ** -0.5).then_inc(a.s_p, 1)
                return step

            def pts(a, hf):
                def step(n):
                    act.wait_ge(a.s_pt, 2 * n + 1 + hf)
                    act.copy(a.PT[:, hf * HALF:(hf + 1) * HALF], a.X[:, :]).then_inc(a.s_pts, 1)
                return step

            def zts(a):
                def step(n):
                    act.wait_ge(a.s_zt, n + 1)
                    act.copy(a.zT[:].rearrange("p a c -> p (a c)"), a.E[:, 0:2 * P]).then_inc(a.s_zts, 1)
                return step

            def h1c(n):
                act.wait_ge(L1.s_out, n + 1)
                act.wait_ge(s_m0, 2 * n + 2)
                if reused(n):
                    act.wait_ge(L3.s_y, n)
                act.copy(x1r[:], h1[:]).then_inc(s_h1c, 1)

            def xts(n):
                act.wait_ge(s_xt, n + 1)
                act.copy(xc[:].rearrange("p a c -> p (a c)"), Bc.X[:, 0:2 * P]).then_inc(s_xts, 1)

            def f1s(n):
                act.wait_ge(s_f1, n + 1)
                act.copy(x2T[:], Bc.X[:, 0:P]).then_inc(s_f1s, 1)

            def f2s(n):
                act.wait_ge(s_f2, n + 1)
                act.activation(hT[:], Bc.E[:, 0:P], ACT.Relu, bias=fc1b_sb[:, 0:1]).then_inc(s_f2s, 1)

            def vs(n):
                for b in range(2):
                    act.wait_ge(C.s_v, 2 * n + 1 + b)
                    if reused(n):
                        act.wait_ge(C.s_vz, 32 * n)
                    act.copy(vst[:, b], C.X[b][:, :]).then_inc(C.s_vs, 1)

            def x3ts(n):
                act.wait_ge(C.s_x3t, n + 1)
                act.copy(x3T[:], C.X[0][:, 0:P]).then_inc(C.s_x3ts, 1)

            def qs(g):
                def step(n):
                    act.wait_ge(C.s_q, 2 * n + 1 + g)
                    for j in range(4):
                        last = act.activation(qT[:, 4 * g + j], C.X[g][:, j * P:(j + 1) * P], ACT.Identity,
                                              bias=bq8[:, 4 * g + j:4 * g + j + 1], scale=float(DK1) ** -0.5)
                    last.then_inc(C.s_qs, 1)
                return step

            def c_exp(g):
                def step(n):
                    act.wait_ge(C.s_sub, 2 * n + 1 + g)
                    act.activation(Pc[:, g * HALF:(g + 1) * HALF], Sc[:, g * HALF:(g + 1) * HALF],
                                   ACT.Exp).then_inc(C.s_p, 1)
                return step

            def c_pts(g):
                def step(n):
                    act.wait_ge(C.s_pt, 2 * n + 1 + g)
                    act.copy(PTc[:, g * HALF:(g + 1) * HALF], C.X[g][:, :]).then_inc(C.s_pts, 1)
                return step

            def cts(g):
                def step(n):
                    act.wait_ge(C.s_ct, 2 * n + 1 + g)
                    act.copy(ctxTs[:, 4 * g:4 * g + 4].rearrange("p a c -> p (a c)"), C.X[g][:, :]).then_inc(C.s_cts, 1)
                return step

            steps = {"B.h1c": h1c, "B.xts": xts, "B.f1s": f1s, "B.f2s": f2s, "C.vs": vs, "C.x3ts": x3ts}
            for nm, a in (("A", A), ("B", Bc)):
                steps |= {nm + ".qk": qk(a), nm + ".exp_0": exp(a, 0), nm + ".exp_1": exp(a, 1),
                          nm + ".pts_0": pts(a, 0), nm + ".pts_1": pts(a, 1), nm + ".zts": zts(a)}
            for g in range(2):
                steps |= {f"C.qs_{g}": qs(g), f"C.exp_{g}": c_exp(g), f"C.pts_{g}": c_pts(g), f"C.cts_{g}": cts(g)}
            act.wait_ge(w_block0, 16 * 10)
            act.wait_ge(ready, 7)
            run(act, steps, ENG)

        @block.vector
        def _(dve):
            tt, ts = dve.tensor_tensor, dve.tensor_scalar
            dve.wait_ge(w_self, 16 * 4)
            dve.tensor_copy(bones[:], at["blockones"]).then_inc(ready, 1)
            ts(bigid[:], ident, BIG, None, ALU.mult).then_inc(ready, 1)
            dve.tensor_copy(iota[:].rearrange("p t h -> p (t h)"), at["iota"]).then_inc(ready, 1)
            dve.memset(A.V[:], 0.0).then_inc(ready, 1)
            dve.memset(Bc.V[:], 0.0).then_inc(ready, 1)
            dve.wait_ge(ready, 5)
            for a in (A, Bc):
                last = dve.tensor_copy(a.V[:, :, :, DK0:DK0 + 1].rearrange("p b (j l) o -> p (b j) (l o)", l=2),
                                       at["vmask"].rearrange("p (j l k) -> p j l k", l=2, k=DK0)[:, :, :, 0]
                                       [:, 0:1].to_broadcast([P, 2 * J, 2]))
            last.then_inc(ready, 1)

            def q0(a):
                def step(n):
                    dve.wait_ge(a.s_qk, n + 1)
                    for b in range(2):
                        ts(a.q0[:, b], at["hmask"], a.qk[:, 0, S * b:S * b + 1], None, ALU.mult).then_inc(a.s_q0, 1)
                return step

            def v(a):
                def step(n):
                    dve.wait_ge(a.s_qk, n + 1)
                    for b in range(2):
                        tt(a.V[:, b, :, 0:DK0], a.X[:, (2 + b) * P:(3 + b) * P].rearrange("p (h k) -> p h k", k=DK0),
                           at["vmask"].rearrange("p (h k) -> p h k", k=DK0), ALU.mult).then_inc(a.s_v, 1)
                return step

            def nz(a):
                def step(n):
                    dve.wait_ge(a.s_e0, n + 1)
                    ts(a.nz[:], a.E[:, 0:H], 0.0, None, ALU.not_equal).then_inc(a.s_nz, 1)
                return step

            def thr(a, causal):
                def step(n):
                    dve.wait_ge(a.s_cnt, n + 1)
                    if causal:
                        ts(a.thr[:], a.E[:, H:2 * H], at["row1"], None, ALU.min).then_inc(a.s_thr, 1)
                    else:
                        dve.tensor_copy(a.thr[:], a.E[:, H:2 * H]).then_inc(a.s_thr, 1)
                    ts(a.lenpos[:], a.E[:, H:2 * H], 0.0, None, ALU.is_gt).then_inc(a.s_thr, 1)
                    dve.wait_ge(a.s_thr, 2 * n + 1)
                    tt(a.mask[:], iota[:], a.thr[:].unsqueeze(1).to_broadcast([P, S, H]),
                       ALU.is_ge).then_inc(a.s_mask, 1)
                return step

            def sub_max(a, hf):
                def step(n):
                    dve.wait_ge(a.s_e, 2 * n + 1 + hf)
                    m = a.mx[:, 8 * hf:8 * hf + 8]
                    dve.tensor_reduce(m, heads(a.E[:, :]), AX.X, ALU.max).then_inc(a.s_max, 1)
                    dve.wait_ge(a.s_max, 2 * n + 1 + hf)
                    tt(heads(a.S[:, hf * HALF:(hf + 1) * HALF]), heads(a.E[:, :]),
                       m.unsqueeze(2).to_broadcast([P, 8, S]), ALU.subtract).then_inc(a.s_sub, 1)
                return step

            def zn(a):
                def step(n):
                    dve.wait_ge(a.s_z, n + 1)
                    zv = a.X[:, 0:2 * P].rearrange("p (h c) -> p h c", c=SLOT)
                    tt(a.den[:], zv[:, :, DK0], a.lenpos[:], ALU.mult).then_inc(a.s_zn, 1)
                    dve.wait_ge(a.s_zn, 3 * n + 1)
                    dve.reciprocal(a.rd[:], a.den[:]).then_inc(a.s_zn, 1)
                    dve.wait_ge(a.s_zn, 3 * n + 2)
                    tt(a.zn[:].rearrange("p (h k) -> p h k", k=DK0), zv[:, :, 0:DK0],
                       a.rd[:].unsqueeze(2).to_broadcast([P, H, DK0]), ALU.mult).then_inc(a.s_zn, 1)
                return step

            def y(a, l, m, res, src=None):
                def step(n):
                    dve.wait_ge(a.s_zn, 3 * n + 3)
                    dve.scalar_tensor_tensor(l.y[:], a.zn[:], m, res, ALU.mult, ALU.add).then_inc(l.s_y, 1)
                return step

            def stats(l):
                def step(n):
                    dve.wait_ge(l.s_y, n + 1)
                    dve.bn_stats(l.st[:], l.y[:]).then_inc(l.s_st, 1)
                    dve.wait_ge(l.s_st, 2 * n + 1)
                    dve.sem_inc(passed, 1)
                    dve.bn_aggr(l.mv[:], l.st[:]).then_inc(l.s_st, 1)
                return step

            def xh(l):
                def step(n):
                    dve.wait_ge(l.s_rstd, 2 * n + 2)
                    ts(l.xh[:], l.y[:], l.mv[:, 0:1], l.rstd[:, 0:1], ALU.subtract, ALU.mult).then_inc(l.s_xh, 1)
                return step

            def m0(n):
                dve.wait_ge(s_xnl, 16 * n + 16)
                if reused(n):
                    dve.wait_ge(s_h1c, n)
                dve.tensor_reduce(A.am[:], A.xn[:], AX.X, ALU.max, apply_absolute_value=True).then_inc(s_m0, 1)
                dve.wait_ge(s_m0, 2 * n + 1)
                ts(h1[:, D:D + 1], A.am[:], 0.0, None, ALU.is_gt).then_inc(s_m0, 1)

            def b_cm(n):
                dve.wait_ge(s_h1c, n + 1)
                dve.wait_ge(s_cnl, 16 * n + 16)
                dve.tensor_reduce(am1[:], x1r[:, 0:D], AX.X, ALU.max, apply_absolute_value=True).then_inc(s_cm, 1)
                dve.wait_ge(s_cm, 3 * n + 1)
                ts(m1[:], am1[:], 0.0, None, ALU.is_gt).then_inc(s_cm, 1)
                dve.wait_ge(s_cm, 3 * n + 2)
                ts(cm[:], cn[:], m1[:, 0:1], None, ALU.mult).then_inc(s_cm, 1)

            def b_y3(n):
                dve.wait_ge(s_f3, n + 1)
                tt(ffn[:], Bc.X[:, 0:P], vec["fc2_b"], ALU.add).then_inc(s_ffn, 1)
                dve.wait_ge(s_ffn, n + 1)
                dve.scalar_tensor_tensor(L3.y[:], ffn[:], x1r[:, D:D + 1], x2[:], ALU.mult, ALU.add
                                         ).then_inc(L3.s_y, 1)

            def ks(n):
                if isinstance(n, int) and n == 0:
                    dve.wait_ge(bvo_ready, 1)
                    tt(obias[:], C.E[0][:, 0:D], vec["bo"], ALU.add).then_inc(bvo_ready, 1)
                for g in range(2):
                    dve.wait_ge(C.s_k, 2 * n + 1 + g)
                    if reused(n):
                        dve.wait_ge(C.s_kz, 32 * n)
                    tt(kst[:, 4 * g:4 * g + 4], C.X[g][:, :].rearrange("p (j t) -> p j t", t=P),
                       bk_sb[:, 4 * g:4 * g + 4].unsqueeze(2).to_broadcast([P, 4, P]), ALU.add).then_inc(C.s_ks, 1)

            def fadd(g):
                def step(n):
                    dve.wait_ge(C.s_e, 2 * n + 1 + g)
                    if g == 0:
                        dve.wait_ge(C.s_fl, 16 * n + 16)
                    sc = Sc[:, g * HALF:(g + 1) * HALF]
                    dve.scalar_tensor_tensor(sc, f[:].rearrange("p h t -> p (h t)")[:, g * HALF:(g + 1) * HALF], 2.0,
                                             C.E[g][:, :], ALU.mult, ALU.add).then_inc(C.s_s, 1)
                    dve.wait_ge(C.s_s, 2 * n + 1 + g)
                    dve.tensor_reduce(mxc[:, 8 * g:8 * g + 8], heads(sc), AX.X, ALU.max).then_inc(C.s_max, 1)
                return step

            def den(g):
                def step(n):
                    dve.wait_ge(C.s_p, 2 * n + 1 + g)
                    d = denc[:, 8 * g:8 * g + 8]
                    dve.tensor_reduce(d, heads(Pc[:, g * HALF:(g + 1) * HALF]), AX.X, ALU.add).then_inc(C.s_den, 1)
                    dve.wait_ge(C.s_den, 2 * n + 1 + g)
                    dve.reciprocal(rdc[:, 8 * g:8 * g + 8], d).then_inc(C.s_rd, 1)
                return step

            def c_cn(g):
                def step(n):
                    dve.wait_ge(C.s_ctx, 2 * n + 1 + g)
                    dve.wait_ge(C.s_rd, 2 * n + 1 + g)
                    tt(heads(ctxs[:, g * HALF:(g + 1) * HALF]), heads(C.E[g][:, :]),
                       rdc[:, 8 * g:8 * g + 8].unsqueeze(2).to_broadcast([P, 8, DK1]), ALU.mult).then_inc(C.s_cn, 1)
                return step

            def c_y(n):
                dve.wait_ge(C.s_o, n + 1)
                dve.wait_ge(C.s_x3r, n + 1)
                tt(L4.y[:], C.E[0][:, 0:D], x3r[:], ALU.add).then_inc(L4.s_y, 1)

            steps = {"A.m0": m0, "B.cm": b_cm, "B.y3": b_y3, "C.ks": ks, "C.y": c_y,
                     "A.thr": thr(A, True), "B.thr": thr(Bc, False),
                     "A.y": y(A, L1, h1[:, D:D + 1], A.xn[:]), "B.y": y(Bc, L2, m1[:, 0:1], x1r[:, 0:D])}
            for k, l in (("A.", L1), ("B.", L2), ("B.3", L3), ("C.", L4)):
                steps |= {k + "st": stats(l), k + "xh": xh(l)}
            for nm, a in (("A", A), ("B", Bc)):
                steps |= {nm + ".q0": q0(a), nm + ".vz": v(a), nm + ".nz": nz(a), nm + ".zn": zn(a),
                          nm + ".max_0": sub_max(a, 0), nm + ".max_1": sub_max(a, 1)}
            for g in range(2):
                steps |= {f"C.fadd_{g}": fadd(g), f"C.den_{g}": den(g), f"C.cn_{g}": c_cn(g)}
            dve.wait_ge(w_block0, 16 * 10)
            ts(bq8[:], bq_sb[:], float(DK1) ** -0.5, None, ALU.mult).then_inc(ready, 1)
            run(dve, steps, ENG)

        @block.gpsimd
        def _(pool):
            tt, ts = pool.tensor_tensor, pool.tensor_scalar
            pool.memset(Kz[:], 0.0).then_inc(zeroed, 1)
            pool.memset(Vz[:], 0.0).then_inc(zeroed, 1)

            def kblk(a):
                def step(n):
                    pool.wait_ge(a.s_qk, n + 1)
                    for hf in range(2):
                        tt(a.kblk[:, 8 * hf:8 * hf + 8], a.qk[:, 1].unsqueeze(1).to_broadcast([P, 8, P]),
                           at["hmask"][:, 8 * hf:8 * hf + 8].unsqueeze(2).to_broadcast([P, 8, P]),
                           ALU.mult).then_inc(a.s_kblk, 1)
                return step

            def rstd(l):
                def step(n):
                    pool.wait_ge(l.s_st, 2 * n + 2)
                    tt(l.ve[:], l.mv[:, 1:2], at[l.eps], ALU.add).then_inc(l.s_rstd, 1)
                    pool.wait_ge(l.s_rstd, 2 * n + 1)
                    tt(l.rstd[:], l.ve[:], at["power"], ALU.pow).then_inc(l.s_rstd, 1)
                return step

            def gb(l, *free):
                def step(n):
                    pool.wait_ge(l.s_xh, n + 1)
                    tt(l.xg[:], l.xh[:], l.g, ALU.mult).then_inc(l.s_xg, 1)
                    pool.wait_ge(l.s_xg, n + 1)
                    if reused(n):
                        for readers, per in free:
                            pool.wait_ge(readers, per * n)
                    tt(l.out, l.xg[:], l.b, ALU.add).then_inc(l.s_out, 1)
                return step

            def x3c(n):
                pool.wait_ge(L3.s_out, n + 1)
                if reused(n):
                    pool.wait_ge(L4.s_y, n)
                if isinstance(n, int) and n == 0:
                    pool.wait_ge(bvo_ready, 2)
                tt(x3r[:], h2[:], obias[:], ALU.add).then_inc(C.s_x3r, 1)

            def c_sub(g):
                def step(n):
                    pool.wait_ge(C.s_max, 2 * n + 1 + g)
                    v = heads(Sc[:, g * HALF:(g + 1) * HALF])
                    tt(v, v, mxc[:, 8 * g:8 * g + 8].unsqueeze(2).to_broadcast([P, 8, S]),
                       ALU.subtract).then_inc(C.s_sub, 1)
                return step

            steps = {"C.x3c": x3c, "C.sub_0": c_sub(0), "C.sub_1": c_sub(1),
                     "A.kblk": kblk(A), "B.kblk": kblk(Bc),
                     "A.gb": gb(L1, (s_h1c, 1)),
                     "B.gb": gb(L2, (L3.s_y, 1)),
                     "B.3gb": gb(L3, (C.s_x3r, 1), (C.s_x3t, 1)),
                     "C.gb": gb(L4, (s_st, 16))}
            for k, l in (("A.", L1), ("B.", L2), ("B.3", L3), ("C.", L4)):
                steps[k + "rstd"] = rstd(l)
            pool.wait_ge(w_self, 16 * 4)
            pool.wait_ge(w_block0, 16 * 10)
            run(pool, steps, ENG)


TURN = """
C.e_1+1 B.q0+2 C.cts_0+0 C.store+0 B.pv+2 C.sub_0+1 B.vz+2 A.pt_1+3 B.z+2 B.f2s+1 C.cts_1+0 B.nz+2 A.pv+3
C.sub_1+1 C.x3c+1 A.vz+3 B.thr+2 B.h1c+2 B.xts+2 C.pt_0+1 B.rstd+2 B.qk+2 B.gb+2 C.pt_1+1 C.vs+1 A.z+3
C.st+0 B.max_0+2 A.max_0+3 B.max_1+2 C.x3ts+1 A.rstd+3 C.xh+0 C.fadd_0+1 A.max_1+3 C.ctx_0+1 C.ctx_1+1
C.fadd_1+1 A.qkv+4 C.den_0+1 B.f1+2 B.zn+2 B.y+2 C.qs_0+1 B.st+2 C.ct_0+1 B.exp_0+2 A.gb+3 A.exp_0+3
C.qs_1+1 B.pts_0+2 C.den_1+1 A.zn+3 B.f2+2 B.exp_1+2 B.xh+2 A.y+3 A.pts_0+3 C.ct_1+1 B.pts_1+2 A.kblk+4
C.cn_0+1 A.e0+4 A.exp_1+3 C.kz+2 B.f3+2 C.exp_0+1 A.st+3 C.cn_1+1 B.zts+2 A.q0+4 A.pts_1+3 A.cnt+4 C.k+2
C.exp_1+1 A.xh+3 A.zts+3 C.pts_0+1 B.3rstd+2 C.vz+2 A.nz+4 B.tr+3 C.o+1 B.3gb+2 C.pts_1+1 B.qkv+3 C.v+2
B.e0+3 C.x3t+2 B.cnt+3 A.e_0+4 B.e_0+3 B.kblk+3 B.y3+2 C.rstd+1 C.q+2 B.e_1+3 B.pt_0+3 B.cm+3 A.m0+4 C.e_0+2
C.gb+1 B.3st+2 A.qk+4 A.e_1+4 C.ks+2 A.pt_0+4 B.3xh+2 C.y+1 B.pt_1+3 B.f1s+2 A.thr+4
"""
ORDER = [(w[0], w[2:].split("+")[0], int(w.split("+")[1])) for w in TURN.split()]
AHEAD = max(k for _, _, k in ORDER)

_OUT = ((B, S, D), "float32")


def kernel(**inputs):
    import concourse.bacc as _bacc
    from concourse.bass_utils import run_bass_kernel_spmd as _run

    g = {k: np.asarray(v) for k, v in inputs.items()}
    L0 = {k[9:]: v for k, v in g.items() if k.startswith("L0_xattn_")}
    L1 = {k[9:]: v for k, v in g.items() if k.startswith("L1_xattn_")}
    T = B * S
    x, c, fs = g["x"], g["ctx_1024"], g["fside_Bx16xSxS2_0"]

    def col(v):
        return v.reshape(J, P).T

    arrays = {
        "consts": constants(),
        "x": x.reshape(T, D), "xT": x.reshape(T, D).T, "ctxn": c.reshape(T, D), "ctxT": c.reshape(T, D).T,
        "fs": fs.transpose(0, 2, 1, 3).reshape(T, H * S),
        **{n: L0[n].transpose(1, 0, 2).reshape(D, D) for n in ("Wq1", "Wk1", "Wv1", "Wq2", "Wk2", "Wv2")},
        "fc1T": L0["fc1_w"].T, "fc2T": L0["fc2_w"].T,
        "vecs": np.stack([L0["ln1_g"], L0["ln1_b"], L0["ln2_g"], L0["ln2_b"], L0["ln3_g"], L0["ln3_b"], L1["ln_g"],
                          L1["ln_b"], L1["bo"], L0["fc2_b"]]),
        "fc1b": L0["fc1_b"].reshape(D, 1),
        "wq": L1["wq"], "wk": L1["wk"], "wv": L1["wv"], "wo": L1["wo"],
        "bq": col(L1["bq"]), "bk": col(L1["bk"]), "bv": col(L1["bv"]),
    }
    nc = _bacc.Bacc("TRN2", target_bir_lowering=False, num_devices=1)
    named, args = {}, []
    for name, a in arrays.items():
        a = np.ascontiguousarray(a)
        named[f"in_{name}"] = a
        args.append(nc.dram_tensor(f"in_{name}", a.shape, mybir.dt.from_np(a.dtype), kind="ExternalInput").ap())
    args.append(nc.dram_tensor("out_0", (T, D), F32, kind="ExternalOutput").ap())
    bass_two_blocks(nc, *args)
    r = _run(nc, [named], core_ids=[0])
    return r.results[0]["out_0"].reshape(_OUT[0])
```

```python
from contextlib import ExitStack

import numpy as np

import concourse.bass as bass
from concourse import mybir

F32 = mybir.dt.float32
BF16 = mybir.dt.bfloat16
ALU = mybir.AluOpType
ACT = mybir.ActivationFunctionType
AX = mybir.AxisListType

P = 128
B, S, D, H = 32, 64, 128, 16
PAIRS = B // 2
DK0 = D // H
DK1 = 64
HD = H * DK1
J = H // 2
HALF = 512
EPS0, EPS1 = 1e-5, 1e-6
BIG = -1e30
SLOT = 16

CONST = dict(ident=P, blockones=P, hmask=H, vmask=P, row1=1, power=1, eps0=1, eps1=1)


def constants():
    p = np.arange(P)
    c = {
        "ident": np.eye(P),
        "blockones": p[:, None] // S == p[None] // S,
        "hmask": p[:, None] // DK0 == np.arange(H)[None],
        "vmask": p[:, None] // S == (np.arange(P)[None] // DK0) % 2,
        "row1": p[:, None] % S + 1,
        "power": np.full((P, 1), -0.5),
        "eps0": np.full((P, 1), EPS0),
        "eps1": np.full((P, 1), EPS1),
    }
    return np.concatenate([c[k].astype(np.float32) for k in CONST], axis=1)


def bass_two_blocks(nc, consts, columns, x, xT, ctxn, ctxT, fs, Wq1, Wk1, Wv1, Wq2, Wk2, Wv2, fc1T, fc2T,
                    vecs, fc1b, wq, wk, wvT, wo, bq, bk, bv, out):
    with ExitStack() as stack:
        def sb(name, shape, dt=F32):
            return stack.enter_context(nc.sbuf_tensor(name, shape, dt))

        def ps(name):
            return stack.enter_context(nc.psum_tensor(name, [P, HALF], F32))

        def sem(name):
            return stack.enter_context(nc.semaphore(name))

        cst = sb("cst", [P, sum(CONST.values())])
        at, cut = {}, 0
        for k, w in CONST.items():
            at[k] = cst[:, cut:cut + w]
            cut += w
        ident = at["ident"]
        bones = sb("bones", [P, P], BF16)
        bigid = sb("bigid", [P, P], BF16)
        iota_f, iota = sb("iota_f", [P, S * H]), sb("iota", [P, S, H], BF16)
        W = {}
        for n in ("Wq1", "Wk1", "Wv1", "Wq2", "Wk2", "Wv2", "fc1T", "fc2T"):
            W[n] = sb(n + "_sb", [P, P])
        wq_sb, wk_sb = sb("wq_sb", [P, HD]), sb("wk_sb", [P, HD])
        wvT_sb, wo_sb = sb("wvT_sb", [P, J, D]), sb("wo_sb", [P, J, D])
        wvo_sb = sb("wvo_sb", [P, 2, J, D])
        VEC = ("ln1_g", "ln1_b", "ln2_g", "ln2_b", "ln3_g", "ln3_b", "ln_g", "ln_b", "bo", "fc2_b")
        vec_sb = sb("vec_sb", [P, len(VEC), D])
        vec = {n: vec_sb[:, k, :] for k, n in enumerate(VEC)}
        fc1b_sb = sb("fc1b_sb", [P, 1])
        bq_sb, bk_sb, bv_sb = (sb(n, [P, J]) for n in ("bq_sb", "bk_sb", "bv_sb"))
        bq8 = sb("bq8", [P, J])
        obias = sb("obias", [P, D])
        w_self, w_columns, w_block0, w_block1, w_fold = (
            sem(n) for n in ("w_self", "w_columns", "w_block0", "w_block1", "w_fold"))
        ready, zeroed = sem("ready"), sem("zeroed")
        bvo_ready, wvo_ready, wvo_copied = sem("bvo_ready"), sem("wvo_ready"), sem("wvo_copied")

        class Ns:
            pass

        def attention(name):
            a = Ns()
            a.E, a.X = ps(name + "_E"), ps(name + "_X")
            a.qk = sb(name + "_qk", [P, 2, P])
            a.kblk = sb(name + "_kblk", [P, H, P])
            a.q0 = sb(name + "_q0", [P, 2, H])
            a.nz = sb(name + "_nz", [P, H], BF16)
            a.thr = sb(name + "_thr", [P, H], BF16)
            a.lenpos = sb(name + "_lenpos", [P, H])
            a.mask = sb(name + "_mask", [P, S, H], BF16)
            a.mx = sb(name + "_mx", [P, H])
            a.S = sb(name + "_S", [P, H * S])
            a.V = sb(name + "_V", [P, 2, H, SLOT])
            a.PT = sb(name + "_PT", [P, H * S])
            a.zT = sb(name + "_zT", [P, 2, P])
            a.den = sb(name + "_den", [P, H])
            a.rd = sb(name + "_rd", [P, H])
            a.zn = sb(name + "_zn", [P, D])
            a.s_qkv = sem(name + "_qkv")
            a.s_qk = sem(name + "_qk")
            a.s_q0 = sem(name + "_q0")
            a.s_v = sem(name + "_v")
            a.s_kblk = sem(name + "_kblk")
            a.s_e0 = sem(name + "_e0")
            a.s_nz = sem(name + "_nz")
            a.s_cnt = sem(name + "_cnt")
            a.s_thr = sem(name + "_thr")
            a.s_mask = sem(name + "_mask")
            a.s_e = sem(name + "_e")
            a.s_max = sem(name + "_max")
            a.s_sub = sem(name + "_sub")
            a.s_p = sem(name + "_p")
            a.s_pt = sem(name + "_pt")
            a.s_pts = sem(name + "_pts")
            a.s_zt = sem(name + "_zt")
            a.s_zts = sem(name + "_zts")
            a.s_z = sem(name + "_z")
            a.s_zn = sem(name + "_zn")
            return a

        def norm(name, g, b, eps, out_ap):
            l = Ns()
            l.y = sb(name + "_y", [P, D])
            l.st = sb(name + "_st", [P, 6])
            l.mv = sb(name + "_mv", [P, 2])
            l.ve = sb(name + "_ve", [P, 1])
            l.rstd = sb(name + "_rstd", [P, 1])
            l.xh = sb(name + "_xh", [P, D])
            l.xg = sb(name + "_xg", [P, D])
            l.g, l.b, l.eps, l.out = vec[g], vec[b], eps, out_ap
            l.s_y, l.s_st, l.s_rstd, l.s_xh, l.s_xg, l.s_out = (
                sem(name + "_" + s) for s in ("y", "st", "rstd", "xh", "xg", "out"))
            return l

        h1 = sb("h1", [P, D + 1])
        h2 = sb("h2", [P, D])
        x2 = sb("x2", [P, D])
        osb = sb("osb", [P, D])
        A, Bc = attention("A"), attention("B")
        L1 = norm("L1", "ln1_g", "ln1_b", "eps0", h1[:, 0:D])
        L2 = norm("L2", "ln2_g", "ln2_b", "eps0", x2[:])
        L3 = norm("L3", "ln3_g", "ln3_b", "eps0", h2[:])
        L4 = norm("L4", "ln_g", "ln_b", "eps1", osb[:])

        A.xT, A.xn, A.am = sb("A_xT", [P, P]), sb("A_xn", [P, D]), sb("A_am", [P, 1])
        s_xTl, s_xnl, s_m0 = sem("s_xTl"), sem("s_xnl"), sem("s_m0")
        x1r = sb("x1r", [P, D + 1])
        cn, cm, xc = sb("cn", [P, D]), sb("cm", [P, D]), sb("xc", [P, 2, P])
        am1, m1 = sb("am1", [P, 1]), sb("m1", [P, 1])
        x2T, hT, ffn = sb("x2T", [P, P]), sb("hT", [P, P]), sb("ffn", [P, D])
        s_cnl, s_h1c, s_cm, s_xt, s_xts = (sem(n) for n in ("s_cnl", "s_h1c", "s_cm", "s_xt", "s_xts"))
        s_f1, s_f1s, s_f2, s_f2s, s_f3, s_ffn = (sem(n) for n in ("s_f1", "s_f1s", "s_f2", "s_f2s", "s_f3", "s_ffn"))
        C = Ns()
        C.E, C.X = [ps("C_E0"), ps("C_E1")], [ps("C_X0"), ps("C_X1")]
        cT, f = sb("cT", [P, P]), sb("f", [P, H, S])
        kst, Kz = sb("kst", [P, J, P]), sb("Kz", [P, 2, J, P])
        VW = sb("VW", [P, 2, J, D])
        x3T, x3r, qT = sb("x3T", [P, P]), sb("x3r", [P, D]), sb("qT", [P, J, P])
        Sc, Pc = sb("Sc", [P, H * S]), sb("Pc", [P, H * S])
        mxc, denc, rdc = sb("mxc", [P, H]), sb("denc", [P, H]), sb("rdc", [P, H])
        PTc = sb("PTc", [P, H * S])
        C.s_cTl = sem("C_cTl")
        C.s_fl = sem("C_fl")
        C.s_k = sem("C_k")
        C.s_ks = sem("C_ks")
        C.s_kz = sem("C_kz")
        C.s_v = sem("C_v")
        C.s_vs = sem("C_vs")
        C.s_x3t = sem("C_x3t")
        C.s_x3ts = sem("C_x3ts")
        C.s_x3r = sem("C_x3r")
        C.s_q = sem("C_q")
        C.s_qs = sem("C_qs")
        C.s_e = sem("C_e")
        C.s_s = sem("C_s")
        C.s_max = sem("C_max")
        C.s_sub = sem("C_sub")
        C.s_p = sem("C_p")
        C.s_den = sem("C_den")
        C.s_rd = sem("C_rd")
        C.s_nrm = sem("C_nrm")
        C.s_pt = sem("C_pt")
        C.s_pts = sem("C_pts")
        C.s_o = sem("C_o")
        s_st = sem("s_stored")
        passed = sem("passed")

        def first_pair(n):
            return isinstance(n, int) and n == 0

        def second_pair(n):
            return isinstance(n, int) and n == 1

        def reused(n):
            return not isinstance(n, int) or n > 0

        def heads(ap):
            return ap.rearrange("p (h t) -> p h t", t=S)

        def run(eng, steps, body_counts):
            first, last = body_counts

            def body(i):
                for chain, step, ahead in ORDER:
                    fn = steps.get(chain + "." + step)
                    n = i + ahead
                    if fn and not (isinstance(n, int) and not 0 <= n < PAIRS):
                        fn(n)

            for i in range(-AHEAD, first):
                body(i)
            with eng.Fori(first, last) as i:
                body(i)
            for i in range(last, PAIRS):
                body(i)

        ENG = (1, PAIRS - AHEAD)
        SPR = (1, PAIRS - AHEAD - 1)

        block = stack.enter_context(nc.Block())

        @block.sync
        def _(sp):
            def pair(ap, n):
                return ap[bass.ds(n * P, P), :]

            def load_x(n):
                if reused(n):
                    sp.wait_ge(A.s_qkv, n)
                sp.dma_start(A.xT[:], xT[:, bass.ds(n * P, P)]).then_inc(s_xTl, 16)
                if reused(n):
                    sp.wait_ge(L1.s_y, n)
                sp.dma_start(A.xn[:], pair(x, n)).then_inc(s_xnl, 16)

            def load_cn(n):
                if reused(n):
                    sp.wait_ge(s_cm, 3 * n)
                sp.dma_start(cn[:], pair(ctxn, n)).then_inc(s_cnl, 16)

            def load_c(n):
                if reused(n):
                    sp.wait_ge(C.s_v, 4 * n)
                sp.dma_start(cT[:], ctxT[:, bass.ds(n * P, P)]).then_inc(C.s_cTl, 16)

            def load_f(n):
                if reused(n):
                    sp.wait_ge(C.s_s, 2 * n)
                sp.dma_start(f[:].rearrange("p h t -> p (h t)"), pair(fs, n)).then_inc(C.s_fl, 16)

            load_x(0)
            for n, ap in (("Wq1", Wq1), ("Wk1", Wk1), ("Wv1", Wv1)):
                sp.dma_start(W[n][:], ap).then_inc(w_self, 16)
            sp.dma_start(cst[:], consts).then_inc(w_self, 16)
            sp.dma_start(iota_f[:], columns.to_broadcast([P, S * H])).then_inc(w_columns, 16)
            for n, ap in (("Wq2", Wq2), ("Wk2", Wk2), ("Wv2", Wv2), ("fc1T", fc1T), ("fc2T", fc2T)):
                sp.dma_start(W[n][:], ap).then_inc(w_block0, 16)
            sp.dma_start(vec_sb[:], vecs.rearrange("(o v) d -> o v d", o=1).to_broadcast([P, len(VEC), D])
                         ).then_inc(w_block0, 16)
            sp.dma_start(fc1b_sb[:], fc1b).then_inc(w_block0, 16)
            load_cn(0)
            for t, ap in ((bq_sb, bq), (bk_sb, bk), (bv_sb, bv)):
                sp.dma_start(t[:], ap).then_inc(w_block0, 16)
            for t, ap in ((wvT_sb, wvT), (wo_sb, wo)):
                sp.dma_start(t[:], ap.rearrange("(j p) d -> p j d", p=P)).then_inc(w_fold, 16)
            for t, ap in ((wk_sb, wk), (wq_sb, wq)):
                sp.dma_start(t[:], ap).then_inc(w_block1, 16)
            load_c(0)
            load_f(0)

            def next_pair(load):
                def step(n):
                    if isinstance(n, int) and n + 1 >= PAIRS:
                        return
                    load(n + 1)
                return step

            def kz(n):
                sp.wait_ge(C.s_ks, 2 * n + 2)
                if reused(n):
                    sp.wait_ge(C.s_e, 2 * n)
                if first_pair(n):
                    sp.wait_ge(zeroed, 1)
                for hl in range(2):
                    r = slice(64 * hl, 64 * hl + 64)
                    sp.dma_start(Kz[r, hl], kst[r]).then_inc(C.s_kz, 16)

            def store(n):
                sp.wait_ge(L4.s_out, n + 1)
                sp.dma_start(pair(out, n), osb[:]).then_inc(s_st, 16)

            run(sp, {"A.loadx": next_pair(load_x), "B.loadc": next_pair(load_cn), "C.loadc": next_pair(load_c),
                     "C.loadf": next_pair(load_f), "C.kz": kz, "C.store": store}, SPR)
            sp.wait_ge(s_st, 16 * PAIRS)

        @block.tensor
        def _(pe):
            mm, tr = nc.tensor.matmul, nc.tensor.transpose

            def fold_weights():
                pe.wait_ge(w_fold, 16 * 2)
                for hl in range(2):
                    r = slice(DK1 * hl, DK1 * hl + DK1)
                    for j in range(J):
                        bank = (C.X, C.E)[hl][j // 4]
                        last = mm(bank[:, (j % 4) * P:(j % 4 + 1) * P], wvT_sb[r, j], wo_sb[r, j], start=True,
                                  stop=True)
                last.then_inc(wvo_ready, 1)

            def qkv(a, wqkv, xq, xkv):
                def step(n):
                    if a is A:
                        pe.wait_ge(s_xTl, 16 * n + 16)
                        if reused(n):
                            pe.wait_ge(A.s_zn, 3 * n)
                    else:
                        pe.wait_ge(s_xts, n + 1)
                        if first_pair(n):
                            pe.wait_ge(w_block0, 16 * 10)
                    mm(a.X[:, 0:P], wqkv[0][:], xq, start=True, stop=True)
                    mm(a.X[:, P:2 * P], wqkv[1][:], xkv, start=True, stop=True)
                    for b in range(2):
                        for r in range(2):
                            last = mm(a.X[S * r:S * r + S, (2 + b) * P:(3 + b) * P], xkv[:, S * b:S * b + S],
                                      wqkv[2][:], start=True, stop=True)
                    last.then_inc(a.s_qkv, 1)
                    if a is A and second_pair(n):
                        fold_weights()
                return step

            def e0(a):
                def step(n):
                    pe.wait_ge(a.s_q0, 2 * n + 2)
                    if reused(n):
                        pe.wait_ge(a.s_zts, n)
                    for b in range(2):
                        last = mm(a.E[S * b:S * b + S, 0:H], a.qk[:, 1, S * b:S * b + S], a.q0[:, b], start=True,
                                  stop=True)
                    last.then_inc(a.s_e0, 1)
                return step

            def cnt(a):
                def step(n):
                    pe.wait_ge(a.s_nz, n + 1)
                    mm(a.E[:, H:2 * H], bones[:], a.nz[:], start=True, stop=True).then_inc(a.s_cnt, 1)
                return step

            def energy(a, hf):
                def step(n):
                    pe.wait_ge(a.s_kblk, 2 * n + 1 + hf)
                    if hf == 0:
                        pe.wait_ge(a.s_thr, 2 * n + 2)
                    else:
                        pe.wait_ge(a.s_sub, 2 * n + 1)
                    for b in range(2):
                        mm(a.E[S * b:S * b + S, :], a.qk[:, 0, S * b:S * b + S],
                           a.kblk[:, 8 * hf:8 * hf + 8, S * b:S * b + S], start=True, stop=False,
                           skip_group_check=True)
                    pe.wait_ge(a.s_mask, n + 1)
                    mm(a.E[:, :], bigid[:], a.mask[:, :, 8 * hf:8 * hf + 8].rearrange("p t h -> p h t"),
                       start=False, stop=True, skip_group_check=True).then_inc(a.s_e, 1)
                return step

            def pt(a, hf):
                def step(n):
                    pe.wait_ge(a.s_p, 2 * n + 1 + hf)
                    if hf == 0:
                        pe.wait_ge(a.s_v, 2 * n + 2)
                    else:
                        pe.wait_ge(a.s_pts, 2 * n + 1)
                    for j in range(4):
                        last = tr(a.X[:, j * P:(j + 1) * P], a.S[:, (4 * hf + j) * P:(4 * hf + j + 1) * P], ident)
                    last.then_inc(a.s_pt, 1)
                return step

            def pv(a, hf):
                def step(n):
                    pe.wait_ge(a.s_pts, 2 * n + 1 + hf)
                    pe.wait_ge(a.s_sub, 2 * n + 2)
                    for j in range(4 * hf, 4 * hf + 4):
                        for b in range(2):
                            q = 32 * (j % 4)
                            c = (j // 4) * P + S * b
                            last = mm(a.E[q:q + 32, c:c + S], a.V[:, b, 2 * j:2 * j + 2].rearrange("p a c -> p (a c)"),
                                      a.PT[:, j * P + S * b:j * P + S * b + S], start=True, stop=True)
                    last.then_inc(a.s_zt, 1)
                return step

            def z(a):
                def step(n):
                    pe.wait_ge(a.s_zts, n + 1)
                    for c in range(2):
                        last = tr(a.X[:, c * P:(c + 1) * P], a.zT[:, c], ident)
                    last.then_inc(a.s_z, 1)
                return step

            def b_tr(n):
                pe.wait_ge(s_cm, 3 * n + 3)
                if reused(n):
                    pe.wait_ge(s_ffn, n)
                tr(Bc.X[:, 0:P], x1r[:, 0:D], ident)
                tr(Bc.X[:, P:2 * P], cm[:], ident).then_inc(s_xt, 1)

            def f1(n):
                pe.wait_ge(L2.s_out, n + 1)
                tr(Bc.X[:, 0:P], x2[:], ident).then_inc(s_f1, 1)

            def f2(n):
                pe.wait_ge(s_f1s, n + 1)
                mm(Bc.E[:, 0:P], W["fc1T"][:], x2T[:], start=True, stop=True).then_inc(s_f2, 1)

            def f3(n):
                pe.wait_ge(s_f2s, n + 1)
                mm(Bc.X[:, 0:P], hT[:], W["fc2T"][:], start=True, stop=True).then_inc(s_f3, 1)

            def c_k(g):
                def step(n):
                    if g == 0:
                        pe.wait_ge(C.s_cTl, 16 * n + 16)
                    if g == 0 and first_pair(n):
                        pe.wait_ge(w_block0, 16 * 10)
                        pe.wait_ge(wvo_copied, 4)
                        for j in range(J):
                            last = mm(C.E[0][:, 0:D], bv_sb[:, j:j + 1].to_broadcast([P, P]), wo_sb[:, j],
                                      start=(j == 0), stop=(j == J - 1))
                        last.then_inc(bvo_ready, 1)
                        pe.wait_ge(w_block1, 16 * 2)
                    if reused(n):
                        pe.wait_ge(C.s_vs, 4 * n)
                    for j in range(4):
                        c = (4 * g + j) * P
                        last = mm(C.X[g][:, j * P:(j + 1) * P], wk_sb[:, c:c + P], cT[:], start=True, stop=True)
                    last.then_inc(C.s_k, 1)
                return step

            def c_v(b, q):
                def step(n):
                    if q == 0:
                        pe.wait_ge(C.s_ks, 2 * n + 1 + b)
                    else:
                        pe.wait_ge(C.s_vs, 4 * n + 1 + b)
                    for hl in range(2):
                        last = mm(C.X[b][S * hl:S * hl + S, :], cT[:, S * b:S * b + S],
                                  wvo_sb[:, hl, 4 * q:4 * q + 4].rearrange("p j d -> p (j d)"), start=True, stop=True)
                    last.then_inc(C.s_v, 1)
                return step

            def c_x3t(n):
                pe.wait_ge(L3.s_out, n + 1)
                if reused(n):
                    pe.wait_ge(L4.s_y, n)
                if first_pair(n):
                    pe.wait_ge(bvo_ready, 2)
                tr(C.E[0][:, 0:P], h2[:], ident).then_inc(C.s_x3t, 1)

            def c_q(g):
                def step(n):
                    pe.wait_ge(C.s_x3ts, n + 1)
                    for j in range(4):
                        c = (4 * g + j) * P
                        last = mm(C.E[g][:, j * P:(j + 1) * P], wq_sb[:, c:c + P], x3T[:], start=True, stop=True)
                    last.then_inc(C.s_q, 1)
                return step

            def c_e(g):
                def step(n):
                    pe.wait_ge(C.s_qs, 2 * n + 1 + g)
                    if g == 0:
                        pe.wait_ge(C.s_kz, 32 * n + 32)
                    for j in range(4):
                        for b in range(2):
                            last = mm(C.E[g][S * b:S * b + S, j * P:(j + 1) * P], qT[:, 4 * g + j, S * b:S * b + S],
                                      Kz[:, :, 4 * g + j, S * b:S * b + S], start=True, stop=True)
                    last.then_inc(C.s_e, 1)
                return step

            def c_pt(g):
                def step(n):
                    pe.wait_ge(C.s_nrm, 2 * n + 1 + g)
                    for j in range(4):
                        c = (4 * g + j) * P
                        last = tr(C.E[g][:, j * P:(j + 1) * P], Pc[:, c:c + P], ident)
                    last.then_inc(C.s_pt, 1)
                return step

            def c_o(g):
                def step(n):
                    pe.wait_ge(C.s_pts, 2 * n + 1 + g)
                    if g == 0:
                        pe.wait_ge(C.s_vs, 4 * n + 4)
                    for j in range(4 * g, 4 * g + 4):
                        for b in range(2):
                            c = j * P + S * b
                            last = mm(C.E[0][S * b:S * b + S, 0:D], PTc[:, c:c + S], VW[:, b, j],
                                      start=(j == 0), stop=(j == J - 1), skip_group_check=True)
                    last.then_inc(C.s_o, 1)
                return step

            steps = {"B.tr": b_tr, "B.f1": f1, "B.f2": f2, "B.f3": f3, "C.x3t": c_x3t,
                     "A.qkv": qkv(A, [W[n] for n in ("Wq1", "Wk1", "Wv1")], A.xT[:], A.xT[:]),
                     "B.qkv": qkv(Bc, [W[n] for n in ("Wq2", "Wk2", "Wv2")], xc[:, 0], xc[:, 1])}
            for g in range(2):
                steps |= {f"C.k_{g}": c_k(g), f"C.v_{g}": c_v(g, 0), f"C.v_{g + 2}": c_v(g, 1),
                          f"C.q_{g}": c_q(g), f"C.e_{g}": c_e(g), f"C.pt_{g}": c_pt(g), f"C.o_{g}": c_o(g)}
            for nm, a in (("A", A), ("B", Bc)):
                steps |= {nm + ".e0": e0(a), nm + ".cnt": cnt(a), nm + ".e_0": energy(a, 0), nm + ".e_1": energy(a, 1),
                          nm + ".pt_0": pt(a, 0), nm + ".pt_1": pt(a, 1), nm + ".pv_0": pv(a, 0), nm + ".pv_1": pv(a, 1), nm + ".z": z(a)}
            pe.wait_ge(w_self, 16 * 4)
            run(pe, steps, ENG)

        @block.scalar
        def _(act):
            def copy_folded():
                act.wait_ge(wvo_ready, 1)
                for hl in range(2):
                    for q in range(2):
                        act.copy(wvo_sb[:, hl, 4 * q:4 * q + 4].rearrange("p j d -> p (j d)"),
                                 (C.X, C.E)[hl][q][:, :]).then_inc(wvo_copied, 1)

            def qk(a):
                def step(n):
                    act.wait_ge(a.s_qkv, n + 1)
                    act.copy(a.qk[:].rearrange("p a c -> p (a c)"), a.X[:, 0:2 * P]).then_inc(a.s_qk, 1)
                    if a is A and second_pair(n):
                        copy_folded()
                return step

            def exp(a, hf):
                def step(n):
                    act.wait_ge(a.s_sub, 2 * n + 1 + hf)
                    v = a.S[:, hf * HALF:(hf + 1) * HALF]
                    act.activation(v, v, ACT.Exp, scale=float(DK0) ** -0.5).then_inc(a.s_p, 1)
                return step

            def pts(a, hf):
                def step(n):
                    act.wait_ge(a.s_pt, 2 * n + 1 + hf)
                    act.copy(a.PT[:, hf * HALF:(hf + 1) * HALF], a.X[:, :]).then_inc(a.s_pts, 1)
                return step

            def zts(a):
                def step(n):
                    act.wait_ge(a.s_zt, 2 * n + 2)
                    act.copy(a.zT[:].rearrange("p a c -> p (a c)"), a.E[:, 0:2 * P]).then_inc(a.s_zts, 1)
                return step

            def h1c(n):
                act.wait_ge(L1.s_out, n + 1)
                act.wait_ge(s_m0, 2 * n + 2)
                if reused(n):
                    act.wait_ge(L3.s_y, n)
                act.copy(x1r[:], h1[:]).then_inc(s_h1c, 1)

            def xts(n):
                act.wait_ge(s_xt, n + 1)
                act.copy(xc[:].rearrange("p a c -> p (a c)"), Bc.X[:, 0:2 * P]).then_inc(s_xts, 1)

            def f1s(n):
                act.wait_ge(s_f1, n + 1)
                act.copy(x2T[:], Bc.X[:, 0:P]).then_inc(s_f1s, 1)

            def f2s(n):
                act.wait_ge(s_f2, n + 1)
                if first_pair(n):
                    act.wait_ge(w_block0, 16 * 10)
                act.activation(hT[:], Bc.E[:, 0:P], ACT.Relu, bias=fc1b_sb[:, 0:1]).then_inc(s_f2s, 1)

            def vs(b, q):
                def step(n):
                    act.wait_ge(C.s_v, 4 * n + 1 + 2 * q + b)
                    if q == 0 and reused(n):
                        act.wait_ge(C.s_o, 2 * n)
                    act.copy(VW[:, b, 4 * q:4 * q + 4].rearrange("p j d -> p (j d)"), C.X[b][:, :]).then_inc(C.s_vs, 1)
                return step

            def x3ts(n):
                act.wait_ge(C.s_x3t, n + 1)
                act.copy(x3T[:], C.E[0][:, 0:P]).then_inc(C.s_x3ts, 1)

            def qs(g):
                def step(n):
                    act.wait_ge(C.s_q, 2 * n + 1 + g)
                    for j in range(4):
                        last = act.activation(qT[:, 4 * g + j], C.E[g][:, j * P:(j + 1) * P], ACT.Identity,
                                              bias=bq8[:, 4 * g + j:4 * g + j + 1], scale=float(DK1) ** -0.5)
                    last.then_inc(C.s_qs, 1)
                return step

            def c_exp(g):
                def step(n):
                    act.wait_ge(C.s_sub, 2 * n + 1 + g)
                    act.activation(Pc[:, g * HALF:(g + 1) * HALF], Sc[:, g * HALF:(g + 1) * HALF],
                                   ACT.Exp).then_inc(C.s_p, 1)
                return step

            def c_pts(g):
                def step(n):
                    act.wait_ge(C.s_pt, 2 * n + 1 + g)
                    act.copy(PTc[:, g * HALF:(g + 1) * HALF], C.E[g][:, :]).then_inc(C.s_pts, 1)
                return step

            steps = {"B.h1c": h1c, "B.xts": xts, "B.f1s": f1s, "B.f2s": f2s, "C.x3ts": x3ts}
            for nm, a in (("A", A), ("B", Bc)):
                steps |= {nm + ".qk": qk(a), nm + ".exp_0": exp(a, 0), nm + ".exp_1": exp(a, 1),
                          nm + ".pts_0": pts(a, 0), nm + ".pts_1": pts(a, 1), nm + ".zts": zts(a)}
            for g in range(2):
                steps |= {f"C.vs_{g}": vs(g, 0), f"C.vs_{g + 2}": vs(g, 1), f"C.qs_{g}": qs(g), f"C.exp_{g}": c_exp(g), f"C.pts_{g}": c_pts(g)}
            run(act, steps, ENG)

        @block.vector
        def _(dve):
            tt, ts = dve.tensor_tensor, dve.tensor_scalar
            dve.memset(A.V[:], 0.0).then_inc(ready, 1)
            dve.memset(Bc.V[:], 0.0).then_inc(ready, 1)
            dve.wait_ge(w_self, 16 * 4)
            dve.wait_ge(ready, 2)
            for a in (A, Bc):
                dve.tensor_copy(a.V[:, :, :, DK0:DK0 + 1].rearrange("p b (j l) o -> p (b j) (l o)", l=2),
                                at["vmask"].rearrange("p (j l k) -> p j l k", l=2, k=DK0)[:, :, :, 0]
                                [:, 0:1].to_broadcast([P, 2 * J, 2]))
            dve.tensor_copy(bones[:], at["blockones"])
            ts(bigid[:], ident, BIG, None, ALU.mult)
            dve.wait_ge(w_columns, 16)
            dve.tensor_copy(iota[:].rearrange("p t h -> p (t h)"), iota_f[:]).then_inc(ready, 1)

            def q0(a):
                def step(n):
                    dve.wait_ge(a.s_qk, n + 1)
                    for b in range(2):
                        ts(a.q0[:, b], at["hmask"], a.qk[:, 0, S * b:S * b + 1], None, ALU.mult).then_inc(a.s_q0, 1)
                return step

            def v(a):
                def step(n):
                    dve.wait_ge(a.s_qk, n + 1)
                    for b in range(2):
                        tt(a.V[:, b, :, 0:DK0], a.X[:, (2 + b) * P:(3 + b) * P].rearrange("p (h k) -> p h k", k=DK0),
                           at["vmask"].rearrange("p (h k) -> p h k", k=DK0), ALU.mult).then_inc(a.s_v, 1)
                return step

            def nz(a):
                def step(n):
                    dve.wait_ge(a.s_e0, n + 1)
                    ts(a.nz[:], a.E[:, 0:H], 0.0, None, ALU.not_equal).then_inc(a.s_nz, 1)
                return step

            def thr(a, causal):
                def step(n):
                    dve.wait_ge(a.s_cnt, n + 1)
                    if causal:
                        ts(a.thr[:], a.E[:, H:2 * H], at["row1"], None, ALU.min).then_inc(a.s_thr, 1)
                    else:
                        dve.tensor_copy(a.thr[:], a.E[:, H:2 * H]).then_inc(a.s_thr, 1)
                    ts(a.lenpos[:], a.E[:, H:2 * H], 0.0, None, ALU.is_gt).then_inc(a.s_thr, 1)
                    dve.wait_ge(a.s_thr, 2 * n + 1)
                    if first_pair(n):
                        dve.wait_ge(ready, 3)
                    tt(a.mask[:], iota[:], a.thr[:].unsqueeze(1).to_broadcast([P, S, H]),
                       ALU.is_ge).then_inc(a.s_mask, 1)
                return step

            def maximum(a, hf):
                def step(n):
                    dve.wait_ge(a.s_e, 2 * n + 1 + hf)
                    m = a.mx[:, 8 * hf:8 * hf + 8]
                    dve.tensor_reduce(m, heads(a.E[:, :]), AX.X, ALU.max).then_inc(a.s_max, 1)
                return step

            def sub(a, hf):
                def step(n):
                    m = a.mx[:, 8 * hf:8 * hf + 8]
                    dve.wait_ge(a.s_max, 2 * n + 1 + hf)
                    tt(heads(a.S[:, hf * HALF:(hf + 1) * HALF]), heads(a.E[:, :]),
                       m.unsqueeze(2).to_broadcast([P, 8, S]), ALU.subtract).then_inc(a.s_sub, 1)
                return step

            def zn(a):
                def step(n):
                    dve.wait_ge(a.s_z, n + 1)
                    zv = a.X[:, 0:2 * P].rearrange("p (h c) -> p h c", c=SLOT)
                    tt(a.den[:], zv[:, :, DK0], a.lenpos[:], ALU.mult).then_inc(a.s_zn, 1)
                    dve.wait_ge(a.s_zn, 3 * n + 1)
                    dve.reciprocal(a.rd[:], a.den[:]).then_inc(a.s_zn, 1)
                    dve.wait_ge(a.s_zn, 3 * n + 2)
                    tt(a.zn[:].rearrange("p (h k) -> p h k", k=DK0), zv[:, :, 0:DK0],
                       a.rd[:].unsqueeze(2).to_broadcast([P, H, DK0]), ALU.mult).then_inc(a.s_zn, 1)
                return step

            def y(a, l, m, res, src=None):
                def step(n):
                    dve.wait_ge(a.s_zn, 3 * n + 3)
                    dve.scalar_tensor_tensor(l.y[:], a.zn[:], m, res, ALU.mult, ALU.add).then_inc(l.s_y, 1)
                return step

            def stats(l):
                def step(n):
                    dve.wait_ge(l.s_y, n + 1)
                    dve.bn_stats(l.st[:], l.y[:]).then_inc(l.s_st, 1)
                    dve.wait_ge(l.s_st, 2 * n + 1)
                    dve.sem_inc(passed, 1)
                    dve.bn_aggr(l.mv[:], l.st[:]).then_inc(l.s_st, 1)
                return step

            def xh(l):
                def step(n):
                    dve.wait_ge(l.s_rstd, 2 * n + 2)
                    ts(l.xh[:], l.y[:], l.mv[:, 0:1], l.rstd[:, 0:1], ALU.subtract, ALU.mult).then_inc(l.s_xh, 1)
                return step

            def m0(n):
                dve.wait_ge(s_xnl, 16 * n + 16)
                if reused(n):
                    dve.wait_ge(s_h1c, n)
                dve.tensor_reduce(A.am[:], A.xn[:], AX.X, ALU.max, apply_absolute_value=True).then_inc(s_m0, 1)
                dve.wait_ge(s_m0, 2 * n + 1)
                ts(h1[:, D:D + 1], A.am[:], 0.0, None, ALU.is_gt).then_inc(s_m0, 1)

            def b_cm(n):
                dve.wait_ge(s_h1c, n + 1)
                dve.wait_ge(s_cnl, 16 * n + 16)
                dve.tensor_reduce(am1[:], x1r[:, 0:D], AX.X, ALU.max, apply_absolute_value=True).then_inc(s_cm, 1)
                dve.wait_ge(s_cm, 3 * n + 1)
                ts(m1[:], am1[:], 0.0, None, ALU.is_gt).then_inc(s_cm, 1)
                dve.wait_ge(s_cm, 3 * n + 2)
                ts(cm[:], cn[:], m1[:, 0:1], None, ALU.mult).then_inc(s_cm, 1)

            def b_y3(n):
                dve.wait_ge(s_f3, n + 1)
                tt(ffn[:], Bc.X[:, 0:P], vec["fc2_b"], ALU.add).then_inc(s_ffn, 1)
                dve.wait_ge(s_ffn, n + 1)
                dve.scalar_tensor_tensor(L3.y[:], ffn[:], x1r[:, D:D + 1], x2[:], ALU.mult, ALU.add
                                         ).then_inc(L3.s_y, 1)

            def ks(g):
                def step(n):
                    if g == 0 and first_pair(n):
                        dve.wait_ge(w_block0, 16 * 10)
                        ts(bq8[:], bq_sb[:], float(DK1) ** -0.5, None, ALU.mult)
                        dve.wait_ge(bvo_ready, 1)
                        tt(obias[:], C.E[0][:, 0:D], vec["bo"], ALU.add).then_inc(bvo_ready, 1)
                    dve.wait_ge(C.s_k, 2 * n + 1 + g)
                    if reused(n):
                        dve.wait_ge(C.s_kz, 32 * n)
                    tt(kst[:, 4 * g:4 * g + 4], C.X[g][:, :].rearrange("p (j t) -> p j t", t=P),
                       bk_sb[:, 4 * g:4 * g + 4].unsqueeze(2).to_broadcast([P, 4, P]), ALU.add).then_inc(C.s_ks, 1)
                return step

            def fadd(g):
                def step(n):
                    dve.wait_ge(C.s_e, 2 * n + 1 + g)
                    if g == 0:
                        dve.wait_ge(C.s_fl, 16 * n + 16)
                    sc = Sc[:, g * HALF:(g + 1) * HALF]
                    dve.scalar_tensor_tensor(sc, f[:].rearrange("p h t -> p (h t)")[:, g * HALF:(g + 1) * HALF], 2.0,
                                             C.E[g][:, :], ALU.mult, ALU.add).then_inc(C.s_s, 1)
                return step

            def c_max(g):
                def step(n):
                    sc = Sc[:, g * HALF:(g + 1) * HALF]
                    dve.wait_ge(C.s_s, 2 * n + 1 + g)
                    dve.tensor_reduce(mxc[:, 8 * g:8 * g + 8], heads(sc), AX.X, ALU.max).then_inc(C.s_max, 1)
                return step

            def den(g):
                def step(n):
                    dve.wait_ge(C.s_p, 2 * n + 1 + g)
                    d = denc[:, 8 * g:8 * g + 8]
                    dve.tensor_reduce(d, heads(Pc[:, g * HALF:(g + 1) * HALF]), AX.X, ALU.add).then_inc(C.s_den, 1)
                    dve.wait_ge(C.s_den, 2 * n + 1 + g)
                    dve.reciprocal(rdc[:, 8 * g:8 * g + 8], d).then_inc(C.s_rd, 1)
                return step

            def nrm(g):
                def step(n):
                    dve.wait_ge(C.s_rd, 2 * n + 1 + g)
                    pr = heads(Pc[:, g * HALF:(g + 1) * HALF])
                    tt(pr, pr, rdc[:, 8 * g:8 * g + 8].unsqueeze(2).to_broadcast([P, 8, S]),
                       ALU.mult).then_inc(C.s_nrm, 1)
                return step

            def c_y(n):
                dve.wait_ge(C.s_o, 2 * n + 2)
                dve.wait_ge(C.s_x3r, n + 1)
                if reused(n):
                    dve.wait_ge(L4.s_xh, n)
                tt(L4.y[:], C.E[0][:, 0:D], x3r[:], ALU.add).then_inc(L4.s_y, 1)

            steps = {"A.m0": m0, "B.cm": b_cm, "B.y3": b_y3, "C.y": c_y,
                     "A.thr": thr(A, True), "B.thr": thr(Bc, False),
                     "A.y": y(A, L1, h1[:, D:D + 1], A.xn[:]), "B.y": y(Bc, L2, m1[:, 0:1], x1r[:, 0:D])}
            for k, l in (("A.", L1), ("B.", L2), ("B.3", L3), ("C.", L4)):
                steps |= {k + "st": stats(l), k + "xh": xh(l)}
            for nm, a in (("A", A), ("B", Bc)):
                steps |= {nm + ".q0": q0(a), nm + ".vz": v(a), nm + ".nz": nz(a), nm + ".zn": zn(a),
                          nm + ".max_0": maximum(a, 0), nm + ".max_1": maximum(a, 1),
                          nm + ".sub_0": sub(a, 0), nm + ".sub_1": sub(a, 1)}
            for g in range(2):
                steps |= {f"C.ks_{g}": ks(g), f"C.fadd_{g}": fadd(g), f"C.max_{g}": c_max(g), f"C.den_{g}": den(g), f"C.nrm_{g}": nrm(g)}
            run(dve, steps, ENG)

        @block.gpsimd
        def _(pool):
            tt, ts = pool.tensor_tensor, pool.tensor_scalar
            pool.memset(Kz[:], 0.0).then_inc(zeroed, 1)

            def kblk(a, hf):
                def step(n):
                    pool.wait_ge(a.s_qk, n + 1)
                    tt(a.kblk[:, 8 * hf:8 * hf + 8], a.qk[:, 1].unsqueeze(1).to_broadcast([P, 8, P]),
                       at["hmask"][:, 8 * hf:8 * hf + 8].unsqueeze(2).to_broadcast([P, 8, P]),
                       ALU.mult).then_inc(a.s_kblk, 1)
                return step

            def rstd(l):
                def step(n):
                    pool.wait_ge(l.s_st, 2 * n + 2)
                    tt(l.ve[:], l.mv[:, 1:2], at[l.eps], ALU.add).then_inc(l.s_rstd, 1)
                    pool.wait_ge(l.s_rstd, 2 * n + 1)
                    tt(l.rstd[:], l.ve[:], at["power"], ALU.pow).then_inc(l.s_rstd, 1)
                return step

            def gb(l, *free):
                def step(n):
                    if first_pair(n):
                        pool.wait_ge(w_block0, 16 * 10)
                    pool.wait_ge(l.s_xh, n + 1)
                    tt(l.xg[:], l.xh[:], l.g, ALU.mult).then_inc(l.s_xg, 1)
                    pool.wait_ge(l.s_xg, n + 1)
                    if reused(n):
                        for readers, per in free:
                            pool.wait_ge(readers, per * n)
                    tt(l.out, l.xg[:], l.b, ALU.add).then_inc(l.s_out, 1)
                return step

            def x3c(n):
                pool.wait_ge(L3.s_out, n + 1)
                if reused(n):
                    pool.wait_ge(L4.s_y, n)
                if first_pair(n):
                    pool.wait_ge(bvo_ready, 2)
                tt(x3r[:], h2[:], obias[:], ALU.add).then_inc(C.s_x3r, 1)

            def c_sub(g):
                def step(n):
                    pool.wait_ge(C.s_max, 2 * n + 1 + g)
                    v = heads(Sc[:, g * HALF:(g + 1) * HALF])
                    tt(v, v, mxc[:, 8 * g:8 * g + 8].unsqueeze(2).to_broadcast([P, 8, S]),
                       ALU.subtract).then_inc(C.s_sub, 1)
                return step

            steps = {"C.x3c": x3c, "C.sub_0": c_sub(0), "C.sub_1": c_sub(1),
                     "A.kblk_0": kblk(A, 0), "A.kblk_1": kblk(A, 1), "B.kblk_0": kblk(Bc, 0), "B.kblk_1": kblk(Bc, 1),
                     "A.gb": gb(L1, (s_h1c, 1)),
                     "B.gb": gb(L2, (L3.s_y, 1)),
                     "B.3gb": gb(L3, (C.s_x3r, 1), (C.s_x3t, 1)),
                     "C.gb": gb(L4, (s_st, 16))}
            for k, l in (("A.", L1), ("B.", L2), ("B.3", L3), ("C.", L4)):
                steps[k + "rstd"] = rstd(l)
            pool.wait_ge(w_self, 16 * 4)
            run(pool, steps, ENG)


TURN = """
C.e_0+1 A.kblk_1+3 A.sub_0+3 B.e_1+2 B.loadc+2 A.pt_1+3 B.3xh+1 A.vz+3 C.vs_0+1 B.pt_0+2 C.e_1+1 A.pv_0+3
A.pv_1+3 A.pts_0+3 C.loadf+0 C.vs_1+1 C.y+0 B.3rstd+1 C.qs_0+1 A.m0+3 B.pv_0+2 B.q0+2 C.st+0 B.pt_1+2 B.nz+2
A.max_1+3 B.thr+2 A.exp_1+3 A.sub_1+3 A.z+3 B.max_0+2 B.exp_0+2 C.v_2+1 B.pv_1+2 B.sub_0+2 B.3gb+1 C.kz+1
C.v_3+1 C.qs_1+1 B.vz+2 B.kblk_0+2 A.pts_1+3 B.z+2 C.fadd_0+1 B.pts_0+2 C.pt_0+1 A.qkv+4 C.max_0+1 C.o_0+1
C.k_0+2 B.max_1+2 C.k_1+2 B.exp_1+2 B.sub_1+2 C.xh+0 A.e0+4 C.rstd+0 C.fadd_1+1 B.f1+2 B.kblk_1+2 C.exp_0+1
A.zts+3 C.max_1+1 A.cnt+4 C.den_0+1 A.zn+3 A.loadx+3 B.pts_1+2 C.sub_0+1 A.y+3 C.nrm_0+1 C.vs_2+1 C.pt_1+1
B.f2+2 C.v_0+2 A.st+3 B.f3+2 C.sub_1+1 C.x3c+1 A.rstd+3 C.gb+0 C.v_1+2 B.rstd+2 B.gb+2 B.zts+2 C.exp_1+1
B.zn+2 B.y+2 B.st+2 A.e_0+4 C.vs_3+1 A.kblk_0+4 C.pts_0+1 B.tr+3 C.loadc+1 C.o_1+1 A.qk+4 B.f1s+2 C.den_1+1
B.f2s+2 B.h1c+3 B.qkv+3 C.pts_1+1 A.e_1+4 B.xts+3 B.xh+2 A.xh+3 A.q0+4 A.gb+3 C.nrm_1+1 C.x3t+2 A.nz+4
C.ks_0+2 C.ks_1+2 B.e0+3 A.pt_0+4 B.qk+3 B.cnt+3 A.exp_0+4 C.q_0+2 C.x3ts+2 B.e_0+3 C.store+0 A.thr+4 B.y3+2
B.3st+2 C.q_1+2 B.cm+3 A.max_0+4
"""
ORDER = [(w[0], w[2:].split("+")[0], int(w.split("+")[1])) for w in TURN.split()]
AHEAD = max(k for _, _, k in ORDER)

_OUT = ((B, S, D), "float32")


def kernel(**inputs):
    import concourse.bacc as _bacc
    from concourse.bass_utils import run_bass_kernel_spmd as _run

    g = {k: np.asarray(v) for k, v in inputs.items()}
    L0 = {k[9:]: v for k, v in g.items() if k.startswith("L0_xattn_")}
    L1 = {k[9:]: v for k, v in g.items() if k.startswith("L1_xattn_")}
    T = B * S
    x, c, fs = g["x"], g["ctx_1024"], g["fside_Bx16xSxS2_0"]

    def col(v):
        return v.reshape(J, P).T

    arrays = {
        "consts": constants(),
        "columns": np.repeat(np.arange(S), H)[None].astype(np.float32),
        "x": x.reshape(T, D), "xT": x.reshape(T, D).T, "ctxn": c.reshape(T, D), "ctxT": c.reshape(T, D).T,
        "fs": fs.transpose(0, 2, 1, 3).reshape(T, H * S),
        **{n: L0[n].transpose(1, 0, 2).reshape(D, D) for n in ("Wq1", "Wk1", "Wv1", "Wq2", "Wk2", "Wv2")},
        "fc1T": L0["fc1_w"].T, "fc2T": L0["fc2_w"].T,
        "vecs": np.stack([L0["ln1_g"], L0["ln1_b"], L0["ln2_g"], L0["ln2_b"], L0["ln3_g"], L0["ln3_b"], L1["ln_g"],
                          L1["ln_b"], L1["bo"], L0["fc2_b"]]),
        "fc1b": L0["fc1_b"].reshape(D, 1),
        "wq": L1["wq"], "wk": L1["wk"], "wvT": L1["wv"].T, "wo": L1["wo"],
        "bq": col(L1["bq"]), "bk": col(L1["bk"]), "bv": col(L1["bv"]),
    }
    nc = _bacc.Bacc("TRN2", target_bir_lowering=False, num_devices=1)
    named, args = {}, []
    for name, a in arrays.items():
        a = np.ascontiguousarray(a)
        named[f"in_{name}"] = a
        args.append(nc.dram_tensor(f"in_{name}", a.shape, mybir.dt.from_np(a.dtype), kind="ExternalInput").ap())
    args.append(nc.dram_tensor("out_0", (T, D), F32, kind="ExternalOutput").ap())
    bass_two_blocks(nc, *args)
    r = _run(nc, [named], core_ids=[0])
    return r.results[0]["out_0"].reshape(_OUT[0])
```

```python
from contextlib import ExitStack

import numpy as np

import concourse.bass as bass
from concourse import mybir

F32 = mybir.dt.float32
BF16 = mybir.dt.bfloat16
F32R = mybir.dt.float32r
ALU = mybir.AluOpType
ACT = mybir.ActivationFunctionType
AX = mybir.AxisListType

P = 128
B, S, D, H = 32, 64, 128, 16
PAIRS = B // 2
DK0 = D // H
DK1 = 64
HD = H * DK1
J = H // 2
HALF = H * S // 2
EPS0, EPS1 = 1e-5, 1e-6
BIG = -1e30
SLOT = 16

CONST = dict(ident=P, blockones=P, hmask=H, vmask=P, row1=1, power=1, eps0=1, eps1=1)


def constants():
    p = np.arange(P)
    c = {
        "ident": np.eye(P),
        "blockones": p[:, None] // S == p[None] // S,
        "hmask": p[:, None] // DK0 == np.arange(H)[None],
        "vmask": p[:, None] // S == (np.arange(P)[None] // DK0) % 2,
        "row1": p[:, None] % S + 1,
        "power": np.full((P, 1), -0.5),
        "eps0": np.full((P, 1), EPS0),
        "eps1": np.full((P, 1), EPS1),
    }
    return np.concatenate([c[k].astype(np.float32) for k in CONST], axis=1)


def bass_two_blocks(nc, consts, columns, x, xT, ctxn, ctxT, fs, Wq1, Wk1, Wv1, Wq2, Wk2, Wv2, fc1T, fc2T,
                    vecs, fc1b, wq, wk, wvT, wo, bq, bk, bv, out):
    with ExitStack() as stack:
        def sb(name, shape, dt=F32):
            return stack.enter_context(nc.sbuf_tensor(name, shape, dt))

        def ps(name):
            return stack.enter_context(nc.psum_tensor(name, [P, HALF], F32))

        def sem(name):
            return stack.enter_context(nc.semaphore(name))

        cst = sb("cst", [P, sum(CONST.values())])
        at, cut = {}, 0
        for k, w in CONST.items():
            at[k] = cst[:, cut:cut + w]
            cut += w
        ident = at["ident"]
        bones = sb("bones", [P, P], BF16)
        bigid = sb("bigid", [P, P], BF16)
        iota_f, iota = sb("iota_f", [P, S * H]), sb("iota", [P, S, H], BF16)
        W = {}
        for n in ("Wq1", "Wk1", "Wv1", "Wq2", "Wk2", "Wv2", "fc1T", "fc2T"):
            W[n] = sb(n + "_sb", [P, P])
        wq_sb, wk_sb = sb("wq_sb", [P, HD]), sb("wk_sb", [P, HD])
        wvT_sb, wo_sb = sb("wvT_sb", [P, J, D]), sb("wo_sb", [P, J, D])
        wvo_hi, wvo_lo = sb("wvo_hi", [P, 2, J, D], F32R), sb("wvo_lo", [P, 2, J, D], F32R)
        VEC = ("ln1_g", "ln1_b", "ln2_g", "ln2_b", "ln3_g", "ln3_b", "ln_g", "ln_b", "bo", "fc2_b")
        vec_sb = sb("vec_sb", [P, len(VEC), D])
        vec = {n: vec_sb[:, k, :] for k, n in enumerate(VEC)}
        fc1b_sb = sb("fc1b_sb", [P, 1])
        bq_sb, bk_sb, bv_sb = (sb(n, [P, J]) for n in ("bq_sb", "bk_sb", "bv_sb"))
        bq8 = sb("bq8", [P, J])
        obias = sb("obias", [P, D])
        w_self, w_columns, w_block0, w_block1, w_fold = (
            sem(n) for n in ("w_self", "w_columns", "w_block0", "w_block1", "w_fold"))
        ready, zeroed = sem("ready"), sem("zeroed")
        bvo_ready, wvo_ready, wvo_high, wvo_split = (
            sem(n) for n in ("bvo_ready", "wvo_ready", "wvo_high", "wvo_split"))

        class Chain:
            pass

        def attention(name):
            a = Chain()
            a.E, a.X = ps(name + "_E"), ps(name + "_X")
            a.qk = sb(name + "_qk", [P, 2, P])
            a.kblk = sb(name + "_kblk", [P, H, P])
            a.q0 = sb(name + "_q0", [P, 2, H])
            a.nz = sb(name + "_nz", [P, H], BF16)
            a.thr = sb(name + "_thr", [P, H], BF16)
            a.lenpos = sb(name + "_lenpos", [P, H])
            a.mask = sb(name + "_mask", [P, S, H], BF16)
            a.mx = sb(name + "_mx", [P, H])
            a.S = sb(name + "_S", [P, H * S])
            a.V = sb(name + "_V", [P, 2, H, SLOT])
            a.PT = sb(name + "_PT", [P, H * S])
            a.zT = sb(name + "_zT", [P, 2, P])
            a.den = sb(name + "_den", [P, H])
            a.rd = sb(name + "_rd", [P, H])
            a.zn = sb(name + "_zn", [P, D])
            a.s_qkv = sem(name + "_qkv")
            a.s_qk = sem(name + "_qk")
            a.s_q0 = sem(name + "_q0")
            a.s_v = sem(name + "_v")
            a.s_kblk = sem(name + "_kblk")
            a.s_e0 = sem(name + "_e0")
            a.s_nz = sem(name + "_nz")
            a.s_cnt = sem(name + "_cnt")
            a.s_thr = sem(name + "_thr")
            a.s_mask = sem(name + "_mask")
            a.s_e = sem(name + "_e")
            a.s_max = sem(name + "_max")
            a.s_sub = sem(name + "_sub")
            a.s_p = sem(name + "_p")
            a.s_pt = sem(name + "_pt")
            a.s_pts = sem(name + "_pts")
            a.s_zt = sem(name + "_zt")
            a.s_zts = sem(name + "_zts")
            a.s_z = sem(name + "_z")
            a.s_zn = sem(name + "_zn")
            return a

        def norm(name, g, b, eps, out_ap):
            l = Chain()
            l.y = sb(name + "_y", [P, D])
            l.st = sb(name + "_st", [P, 6])
            l.mv = sb(name + "_mv", [P, 2])
            l.ve = sb(name + "_ve", [P, 1])
            l.rstd = sb(name + "_rstd", [P, 1])
            l.xh = sb(name + "_xh", [P, D])
            l.xg = sb(name + "_xg", [P, D])
            l.g, l.b, l.eps, l.out = vec[g], vec[b], eps, out_ap
            l.s_y, l.s_st, l.s_rstd, l.s_xh, l.s_xg, l.s_out = (
                sem(name + "_" + s) for s in ("y", "st", "rstd", "xh", "xg", "out"))
            return l

        h1 = sb("h1", [P, D + 1])
        h2 = sb("h2", [P, D])
        x2 = sb("x2", [P, D])
        osb = sb("osb", [P, D])
        A, Bc = attention("A"), attention("B")
        L1 = norm("L1", "ln1_g", "ln1_b", "eps0", h1[:, 0:D])
        L2 = norm("L2", "ln2_g", "ln2_b", "eps0", x2[:])
        L3 = norm("L3", "ln3_g", "ln3_b", "eps0", h2[:])
        L4 = norm("L4", "ln_g", "ln_b", "eps1", osb[:])

        A.xT, A.xn, A.am = sb("A_xT", [P, P]), sb("A_xn", [P, D]), sb("A_am", [P, 1])
        s_xTl, s_xnl, s_m0 = sem("s_xTl"), sem("s_xnl"), sem("s_m0")
        x1r = sb("x1r", [P, D + 1])
        cn, cm, xc = sb("cn", [P, D]), sb("cm", [P, D]), sb("xc", [P, 2, P])
        am1, m1, m0r = sb("am1", [P, 1]), sb("m1", [P, 1]), sb("m0r", [P, 1])
        s_m0r = sem("s_m0r")
        x2T, hT, ffn = sb("x2T", [P, P]), sb("hT", [P, P]), sb("ffn", [P, D])
        s_cnl, s_h1c, s_cm, s_xt, s_xts = (sem(n) for n in ("s_cnl", "s_h1c", "s_cm", "s_xt", "s_xts"))
        s_f1, s_f1s, s_f2, s_f2s, s_f3, s_ffn = (sem(n) for n in ("s_f1", "s_f1s", "s_f2", "s_f2s", "s_f3", "s_ffn"))
        C = Chain()
        C.E, C.X = [ps("C_E0"), ps("C_E1")], [ps("C_X0"), ps("C_X1")]
        cT, f = sb("cT", [P, P]), sb("f", [P, H, S])
        kst, Kz = sb("kst", [P, J, P]), sb("Kz", [P, 2, J, P])
        cT_hi, cT_lo = sb("cT_hi", [P, P], F32R), sb("cT_lo", [P, P], F32R)
        vst, VW = sb("vst", [P, 2, J, D]), sb("VW", [P, 2, J, D])
        x3T, x3r, qT = sb("x3T", [P, P]), sb("x3r", [P, D]), sb("qT", [P, J, P])
        Sc, Pc = sb("Sc", [P, H * S]), sb("Pc", [P, H * S])
        mxc, denc, rdc = sb("mxc", [P, H]), sb("denc", [P, H]), sb("rdc", [P, H])
        PTc = sb("PTc", [P, H * S])
        C.s_cTl = sem("C_cTl")
        C.s_fl = sem("C_fl")
        C.s_k = sem("C_k")
        C.s_ks = sem("C_ks")
        C.s_kz = sem("C_kz")
        C.s_v = sem("C_v")
        C.s_vs = sem("C_vs")
        C.s_vz = sem("C_vz")
        C.s_chi = sem("C_chi")
        C.s_clo = sem("C_clo")
        C.s_x3t = sem("C_x3t")
        C.s_x3ts = sem("C_x3ts")
        C.s_x3r = sem("C_x3r")
        C.s_q = sem("C_q")
        C.s_qs = sem("C_qs")
        C.s_e = sem("C_e")
        C.s_s = sem("C_s")
        C.s_max = sem("C_max")
        C.s_sub = sem("C_sub")
        C.s_p = sem("C_p")
        C.s_den = sem("C_den")
        C.s_rd = sem("C_rd")
        C.s_nrm = sem("C_nrm")
        C.s_pt = sem("C_pt")
        C.s_pts = sem("C_pts")
        C.s_o = sem("C_o")
        s_st = sem("s_stored")
        passed, sp_passed = sem("passed"), sem("sp_passed")

        def first_pair(n):
            return isinstance(n, int) and n == 0

        def reused(n):
            return not isinstance(n, int) or n > 0

        def heads(ap):
            return ap.rearrange("p (h t) -> p h t", t=S)

        def run(eng, steps, body_counts):
            first, last = body_counts

            def body(i):
                for chain, step, ahead in ORDER:
                    fn = steps.get(chain + "." + step)
                    n = i + ahead
                    if fn and not (isinstance(n, int) and not 0 <= n < PAIRS):
                        fn(n)

            for i in range(-AHEAD, first):
                body(i)
            with eng.Fori(first, last) as i:
                body(i)
            for i in range(last, PAIRS):
                body(i)

        ENG = (1, PAIRS - AHEAD)
        SPR = (1, PAIRS - AHEAD - 1)

        block = stack.enter_context(nc.Block())

        @block.sync
        def _(sp):
            def pair(ap, n):
                return ap[bass.ds(n * P, P), :]

            def load_x(n):
                if reused(n):
                    sp.wait_ge(A.s_qkv, n)
                sp.dma_start(A.xT[:], xT[:, bass.ds(n * P, P)]).then_inc(s_xTl, 16)
                if reused(n):
                    sp.wait_ge(L1.s_y, n)
                sp.dma_start(A.xn[:], pair(x, n)).then_inc(s_xnl, 16)

            def load_cn(n):
                if reused(n):
                    sp.wait_ge(s_cm, 3 * n)
                sp.dma_start(cn[:], pair(ctxn, n)).then_inc(s_cnl, 16)

            def load_c(n):
                if reused(n):
                    sp.wait_ge(C.s_v, 4 * n)
                    sp.sem_inc(sp_passed, 1)
                sp.dma_start(cT[:], ctxT[:, bass.ds(n * P, P)]).then_inc(C.s_cTl, 16)

            def load_f(n):
                if reused(n):
                    sp.wait_ge(C.s_s, 2 * n)
                sp.dma_start(f[:].rearrange("p h t -> p (h t)"), pair(fs, n)).then_inc(C.s_fl, 16)

            load_x(0)
            for n, ap in (("Wq1", Wq1), ("Wk1", Wk1), ("Wv1", Wv1)):
                sp.dma_start(W[n][:], ap).then_inc(w_self, 16)
            sp.dma_start(cst[:], consts).then_inc(w_self, 16)
            sp.dma_start(iota_f[:], columns.to_broadcast([P, S * H])).then_inc(w_columns, 16)
            for t, ap in ((wvT_sb, wvT), (wo_sb, wo)):
                sp.dma_start(t[:], ap.rearrange("(j p) d -> p j d", p=P)).then_inc(w_fold, 16)
            for n, ap in (("Wq2", Wq2), ("Wk2", Wk2), ("Wv2", Wv2), ("fc1T", fc1T), ("fc2T", fc2T)):
                sp.dma_start(W[n][:], ap).then_inc(w_block0, 16)
            sp.dma_start(vec_sb[:], vecs.rearrange("(o v) d -> o v d", o=1).to_broadcast([P, len(VEC), D])
                         ).then_inc(w_block0, 16)
            sp.dma_start(fc1b_sb[:], fc1b).then_inc(w_block0, 16)
            load_cn(0)
            for t, ap in ((bq_sb, bq), (bk_sb, bk), (bv_sb, bv)):
                sp.dma_start(t[:], ap).then_inc(w_block0, 16)
            for t, ap in ((wk_sb, wk), (wq_sb, wq)):
                sp.dma_start(t[:], ap).then_inc(w_block1, 16)
            load_c(0)
            load_f(0)

            def next_pair(load):
                def step(n):
                    if isinstance(n, int) and n + 1 >= PAIRS:
                        return
                    load(n + 1)
                return step

            def kz(n):
                sp.wait_ge(C.s_ks, 2 * n + 2)
                if reused(n):
                    sp.wait_ge(C.s_e, 2 * n)
                if first_pair(n):
                    sp.wait_ge(zeroed, 1)
                for hl in range(2):
                    r = slice(64 * hl, 64 * hl + 64)
                    sp.dma_start(Kz[r, hl], kst[r]).then_inc(C.s_kz, 16)

            def vz(n):
                if reused(n):
                    sp.wait_ge(C.s_o, 2 * n)
                sp.wait_ge(C.s_vs, 4 * n + 4)
                for hl in range(2):
                    for b in range(2):
                        sp.dma_start(VW[S * hl:S * hl + S, b], vst[S * b:S * b + S, hl]).then_inc(C.s_vz, 16)

            def store(n):
                sp.wait_ge(L4.s_out, n + 1)
                sp.dma_start(pair(out, n), osb[:]).then_inc(s_st, 16)

            run(sp, {"A.loadx": next_pair(load_x), "B.loadc": next_pair(load_cn), "C.loadc": next_pair(load_c),
                     "C.loadf": next_pair(load_f), "C.kz": kz, "C.vz": vz, "C.store": store}, SPR)
            sp.wait_ge(s_st, 16 * PAIRS)

        @block.tensor
        def _(pe):
            mm, tr = nc.tensor.matmul, nc.tensor.transpose

            def fold_weights(part):
                if part == 0:
                    pe.wait_ge(w_fold, 16 * 2)
                hl, q = part // 2, part % 2
                r = slice(DK1 * hl, DK1 * hl + DK1)
                for j in range(4):
                    last = mm((C.X, C.E)[hl][q][:, j * P:(j + 1) * P], wvT_sb[r, 4 * q + j], wo_sb[r, 4 * q + j],
                              start=True, stop=True)
                last.then_inc(wvo_ready, 1)

            def qkv(a, wqkv, xq, xkv):
                def step(n):
                    if a is A:
                        pe.wait_ge(s_xTl, 16 * n + 16)
                        if reused(n):
                            pe.wait_ge(A.s_zn, 3 * n)
                    else:
                        pe.wait_ge(s_xts, n + 1)
                        if first_pair(n):
                            pe.wait_ge(w_block0, 16 * 10)
                    mm(a.X[:, 0:P], wqkv[0][:], xq, start=True, stop=True)
                    mm(a.X[:, P:2 * P], wqkv[1][:], xkv, start=True, stop=True)
                    for b in range(2):
                        for r in range(2):
                            last = mm(a.X[S * r:S * r + S, (2 + b) * P:(3 + b) * P], xkv[:, S * b:S * b + S],
                                      wqkv[2][:], start=True, stop=True)
                    last.then_inc(a.s_qkv, 1)
                return step

            def e0(a):
                def step(n):
                    pe.wait_ge(a.s_q0, 2 * n + 2)
                    if reused(n) and a is A:
                        pe.wait_ge(A.s_zts, n)
                    if reused(n) and a is Bc:
                        pe.wait_ge(s_ffn, n)
                    for b in range(2):
                        last = mm(a.E[S * b:S * b + S, 0:H], a.qk[:, 1, S * b:S * b + S], a.q0[:, b], start=True,
                                  stop=True)
                    last.then_inc(a.s_e0, 1)
                return step

            def cnt(a):
                def step(n):
                    pe.wait_ge(a.s_nz, n + 1)
                    mm(a.E[:, H:2 * H], bones[:], a.nz[:], start=True, stop=True).then_inc(a.s_cnt, 1)
                return step

            def energy(a, hf):
                def step(n):
                    pe.wait_ge(a.s_kblk, 2 * n + 1 + hf)
                    if hf == 0:
                        pe.wait_ge(a.s_thr, 2 * n + 2)
                    else:
                        pe.wait_ge(a.s_sub, 2 * n + 1)
                    for b in range(2):
                        mm(a.E[S * b:S * b + S, :], a.qk[:, 0, S * b:S * b + S],
                           a.kblk[:, 8 * hf:8 * hf + 8, S * b:S * b + S], start=True, stop=False,
                           skip_group_check=True)
                    pe.wait_ge(a.s_mask, n + 1)
                    mm(a.E[:, :], bigid[:], a.mask[:, :, 8 * hf:8 * hf + 8].rearrange("p t h -> p h t"),
                       start=False, stop=True, skip_group_check=True).then_inc(a.s_e, 1)
                    if a is A and first_pair(n):
                        fold_weights(hf)
                return step

            def pt(a, hf):
                def step(n):
                    pe.wait_ge(a.s_p, 2 * n + 1 + hf)
                    if hf == 0:
                        pe.wait_ge(a.s_v, 2 * n + 2)
                    else:
                        pe.wait_ge(a.s_pts, 2 * n + 1)
                    for j in range(4):
                        last = tr(a.X[:, j * P:(j + 1) * P], a.S[:, (4 * hf + j) * P:(4 * hf + j + 1) * P], ident)
                    last.then_inc(a.s_pt, 1)
                    if a is A and first_pair(n):
                        fold_weights(2 + hf)
                return step

            def pv(a, hf):
                def step(n):
                    pe.wait_ge(a.s_pts, 2 * n + 1 + hf)
                    pe.wait_ge(a.s_sub, 2 * n + 2)
                    for j in range(4 * hf, 4 * hf + 4):
                        for b in range(2):
                            q = 32 * (j % 4)
                            c = (j // 4) * P + S * b
                            last = mm(a.E[q:q + 32, c:c + S], a.V[:, b, 2 * j:2 * j + 2].rearrange("p a c -> p (a c)"),
                                      a.PT[:, j * P + S * b:j * P + S * b + S], start=True, stop=True)
                    last.then_inc(a.s_zt, 1)
                return step

            def z(a):
                def step(n):
                    pe.wait_ge(a.s_zts, n + 1)
                    for c in range(2):
                        last = tr(a.X[:, c * P:(c + 1) * P], a.zT[:, c], ident)
                    last.then_inc(a.s_z, 1)
                return step

            def b_tr(n):
                pe.wait_ge(s_cm, 3 * n + 3)
                if reused(n):
                    pe.wait_ge(Bc.s_zn, 3 * n)
                tr(Bc.X[:, 0:P], x1r[:, 0:D], ident)
                tr(Bc.X[:, P:2 * P], cm[:], ident).then_inc(s_xt, 1)

            def f1(n):
                pe.wait_ge(L2.s_out, n + 1)
                tr(Bc.E[:, 0:P], x2[:], ident).then_inc(s_f1, 1)

            def f2(n):
                pe.wait_ge(s_f1s, n + 1)
                mm(Bc.E[:, P:2 * P], W["fc1T"][:], x2T[:], start=True, stop=True).then_inc(s_f2, 1)

            def f3(n):
                pe.wait_ge(s_f2s, n + 1)
                mm(Bc.E[:, 2 * P:3 * P], hT[:], W["fc2T"][:], start=True, stop=True).then_inc(s_f3, 1)

            def c_k(g):
                def step(n):
                    if g == 0:
                        pe.wait_ge(C.s_cTl, 16 * n + 16)
                    if g == 0 and first_pair(n):
                        pe.wait_ge(w_block0, 16 * 10)
                        pe.wait_ge(wvo_split, 4)
                        for j in range(J):
                            last = mm(C.X[1][:, 0:D], bv_sb[:, j:j + 1].to_broadcast([P, P]), wo_sb[:, j],
                                      start=(j == 0), stop=(j == J - 1))
                        last.then_inc(bvo_ready, 1)
                        pe.wait_ge(w_block1, 16 * 2)
                    if reused(n):
                        pe.wait_ge(C.s_vs, 4 * n)
                    if g == 1:
                        pe.wait_ge(C.s_ks, 2 * n + 1)
                    for j in range(4):
                        c = (4 * g + j) * P
                        last = mm(C.X[0][:, j * P:(j + 1) * P], wk_sb[:, c:c + P], cT[:], start=True, stop=True)
                    last.then_inc(C.s_k, 1)
                return step

            def c_v(m):
                hl, q = m // 2, m % 2

                def step(n):
                    pe.wait_ge(C.s_clo, n + 1)
                    if m == 0:
                        pe.wait_ge(C.s_ks, 2 * n + 2)
                    else:
                        pe.wait_ge(C.s_vs, 4 * n + m)
                    hi, lo = (w[:, hl, 4 * q:4 * q + 4].rearrange("p j d -> p (j d)") for w in (wvo_hi, wvo_lo))
                    mm(C.X[0][:, :], cT_hi[:], hi, start=True, stop=False)
                    mm(C.X[0][:, :], cT_hi[:], lo, start=False, stop=False)
                    mm(C.X[0][:, :], cT_lo[:], hi, start=False, stop=True).then_inc(C.s_v, 1)
                return step

            def c_x3t(n):
                pe.wait_ge(L3.s_out, n + 1)
                if reused(n):
                    pe.wait_ge(C.s_pts, 2 * n)
                if first_pair(n):
                    pe.wait_ge(wvo_split, 4)
                tr(C.E[0][:, 0:P], h2[:], ident).then_inc(C.s_x3t, 1)

            def c_q(g):
                def step(n):
                    pe.wait_ge(C.s_x3ts, n + 1)
                    for j in range(4):
                        c = (4 * g + j) * P
                        last = mm(C.E[g][:, j * P:(j + 1) * P], wq_sb[:, c:c + P], x3T[:], start=True, stop=True)
                    last.then_inc(C.s_q, 1)
                return step

            def c_e(g):
                def step(n):
                    pe.wait_ge(C.s_qs, 2 * n + 1 + g)
                    if g == 0:
                        pe.wait_ge(C.s_kz, 32 * n + 32)
                    for j in range(4):
                        for b in range(2):
                            last = mm(C.E[g][S * b:S * b + S, j * P:(j + 1) * P], qT[:, 4 * g + j, S * b:S * b + S],
                                      Kz[:, :, 4 * g + j, S * b:S * b + S], start=True, stop=True)
                    last.then_inc(C.s_e, 1)
                return step

            def c_pt(g):
                def step(n):
                    pe.wait_ge(C.s_nrm, 2 * n + 1 + g)
                    for j in range(4):
                        c = (4 * g + j) * P
                        last = tr(C.E[g][:, j * P:(j + 1) * P], Pc[:, c:c + P], ident)
                    last.then_inc(C.s_pt, 1)
                return step

            def c_o(g):
                def step(n):
                    pe.wait_ge(C.s_pts, 2 * n + 1 + g)
                    if g == 0:
                        pe.wait_ge(C.s_vz, 64 * n + 64)
                        if reused(n):
                            pe.wait_ge(L4.s_y, n)
                        if first_pair(n):
                            pe.wait_ge(bvo_ready, 2)
                    for j in range(4 * g, 4 * g + 4):
                        for b in range(2):
                            c = j * P + S * b
                            last = mm(C.X[1][S * b:S * b + S, 0:D], PTc[:, c:c + S], VW[:, b, j],
                                      start=(j == 0), stop=(j == J - 1), skip_group_check=True)
                    last.then_inc(C.s_o, 1)
                return step

            steps = {"B.tr": b_tr, "B.f1": f1, "B.f2": f2, "B.f3": f3, "C.x3t": c_x3t,
                     "A.qkv": qkv(A, [W[n] for n in ("Wq1", "Wk1", "Wv1")], A.xT[:], A.xT[:]),
                     "B.qkv": qkv(Bc, [W[n] for n in ("Wq2", "Wk2", "Wv2")], xc[:, 0], xc[:, 1])}
            for g in range(2):
                steps |= {f"C.k_{g}": c_k(g), f"C.v_{g}": c_v(g), f"C.v_{g + 2}": c_v(g + 2),
                          f"C.q_{g}": c_q(g), f"C.e_{g}": c_e(g), f"C.pt_{g}": c_pt(g), f"C.o_{g}": c_o(g)}
            for nm, a in (("A", A), ("B", Bc)):
                steps |= {nm + ".e0": e0(a), nm + ".cnt": cnt(a), nm + ".e_0": energy(a, 0), nm + ".e_1": energy(a, 1),
                          nm + ".pt_0": pt(a, 0), nm + ".pt_1": pt(a, 1),
                          nm + ".pv_0": pv(a, 0), nm + ".pv_1": pv(a, 1), nm + ".z": z(a)}
            pe.wait_ge(w_self, 16 * 4)
            run(pe, steps, ENG)

        @block.scalar
        def _(act):
            def copy_folded(part):
                act.wait_ge(wvo_ready, part + 1)
                hl, q = part // 2, part % 2
                act.copy(wvo_hi[:, hl, 4 * q:4 * q + 4].rearrange("p j d -> p (j d)"),
                         (C.X, C.E)[hl][q][:, :]).then_inc(wvo_high, 1)

            def qk(a):
                def step(n):
                    act.wait_ge(a.s_qkv, n + 1)
                    act.copy(a.qk[:].rearrange("p a c -> p (a c)"), a.X[:, 0:2 * P]).then_inc(a.s_qk, 1)
                return step

            def exp(a, hf):
                def step(n):
                    act.wait_ge(a.s_sub, 2 * n + 1 + hf)
                    v = a.S[:, hf * HALF:(hf + 1) * HALF]
                    act.activation(v, v, ACT.Exp, scale=float(DK0) ** -0.5).then_inc(a.s_p, 1)
                    if a is A and first_pair(n):
                        copy_folded(hf)
                return step

            def pts(a, hf):
                def step(n):
                    act.wait_ge(a.s_pt, 2 * n + 1 + hf)
                    act.copy(a.PT[:, hf * HALF:(hf + 1) * HALF], a.X[:, :]).then_inc(a.s_pts, 1)
                    if a is A and first_pair(n):
                        copy_folded(2 + hf)
                return step

            def zts(a):
                def step(n):
                    act.wait_ge(a.s_zt, 2 * n + 2)
                    act.copy(a.zT[:].rearrange("p a c -> p (a c)"), a.E[:, 0:2 * P]).then_inc(a.s_zts, 1)
                return step

            def h1c(n):
                act.wait_ge(L1.s_out, n + 1)
                act.wait_ge(s_m0, 2 * n + 2)
                if reused(n):
                    act.wait_ge(L2.s_y, n)
                act.copy(x1r[:], h1[:]).then_inc(s_h1c, 1)

            def xts(n):
                act.wait_ge(s_xt, n + 1)
                act.copy(xc[:].rearrange("p a c -> p (a c)"), Bc.X[:, 0:2 * P]).then_inc(s_xts, 1)

            def f1s(n):
                act.wait_ge(s_f1, n + 1)
                act.copy(x2T[:], Bc.E[:, 0:P]).then_inc(s_f1s, 1)

            def f2s(n):
                act.wait_ge(s_f2, n + 1)
                if first_pair(n):
                    act.wait_ge(w_block0, 16 * 10)
                act.activation(hT[:], Bc.E[:, P:2 * P], ACT.Relu, bias=fc1b_sb[:, 0:1]).then_inc(s_f2s, 1)

            def chi(n):
                act.wait_ge(C.s_cTl, 16 * n + 16)
                if reused(n):
                    act.wait_ge(C.s_v, 4 * n)
                act.copy(cT_hi[:], cT[:]).then_inc(C.s_chi, 1)

            def vs(m):
                hl, q = m // 2, m % 2

                def step(n):
                    act.wait_ge(C.s_v, 4 * n + 1 + m)
                    if m == 0 and reused(n):
                        act.wait_ge(C.s_vz, 64 * n)
                    act.copy(vst[:, hl, 4 * q:4 * q + 4].rearrange("p j d -> p (j d)"), C.X[0][:, :]
                             ).then_inc(C.s_vs, 1)
                return step

            def x3ts(n):
                act.wait_ge(C.s_x3t, n + 1)
                act.copy(x3T[:], C.E[0][:, 0:P]).then_inc(C.s_x3ts, 1)

            def qs(g):
                def step(n):
                    act.wait_ge(C.s_q, 2 * n + 1 + g)
                    for j in range(4):
                        last = act.activation(qT[:, 4 * g + j], C.E[g][:, j * P:(j + 1) * P], ACT.Identity,
                                              bias=bq8[:, 4 * g + j:4 * g + j + 1], scale=float(DK1) ** -0.5)
                    last.then_inc(C.s_qs, 1)
                return step

            def c_exp(g):
                def step(n):
                    act.wait_ge(C.s_sub, 2 * n + 1 + g)
                    act.activation(Pc[:, g * HALF:(g + 1) * HALF], Sc[:, g * HALF:(g + 1) * HALF],
                                   ACT.Exp).then_inc(C.s_p, 1)
                return step

            def c_pts(g):
                def step(n):
                    act.wait_ge(C.s_pt, 2 * n + 1 + g)
                    if reused(n):
                        act.wait_ge(C.s_o, 2 * n)
                    act.copy(PTc[:, g * HALF:(g + 1) * HALF], C.E[g][:, :]).then_inc(C.s_pts, 1)
                return step

            steps = {"B.h1c": h1c, "B.xts": xts, "B.f1s": f1s, "B.f2s": f2s, "C.x3ts": x3ts, "C.chi": chi}
            for nm, a in (("A", A), ("B", Bc)):
                steps |= {nm + ".qk": qk(a), nm + ".exp_0": exp(a, 0), nm + ".exp_1": exp(a, 1),
                          nm + ".pts_0": pts(a, 0), nm + ".pts_1": pts(a, 1), nm + ".zts": zts(a)}
            for g in range(2):
                steps |= {f"C.vs_{g}": vs(g), f"C.vs_{g + 2}": vs(g + 2), f"C.qs_{g}": qs(g),
                          f"C.exp_{g}": c_exp(g), f"C.pts_{g}": c_pts(g)}
            run(act, steps, ENG)

        @block.vector
        def _(dve):
            tt, ts = dve.tensor_tensor, dve.tensor_scalar
            dve.memset(A.V[:], 0.0).then_inc(ready, 1)
            dve.memset(Bc.V[:], 0.0).then_inc(ready, 1)
            dve.wait_ge(w_self, 16 * 4)
            dve.wait_ge(ready, 2)
            for a in (A, Bc):
                dve.tensor_copy(a.V[:, :, :, DK0:DK0 + 1].rearrange("p b (j l) o -> p (b j) (l o)", l=2),
                                at["vmask"].rearrange("p (j l k) -> p j l k", l=2, k=DK0)[:, :, :, 0]
                                [:, 0:1].to_broadcast([P, 2 * J, 2]))
            dve.tensor_copy(bones[:], at["blockones"])
            ts(bigid[:], ident, BIG, None, ALU.mult)
            dve.wait_ge(w_columns, 16)
            dve.tensor_copy(iota[:].rearrange("p t h -> p (t h)"), iota_f[:]).then_inc(ready, 1)

            def split_folded():
                for hl in range(2):
                    for q in range(2):
                        dve.wait_ge(wvo_high, 2 * hl + q + 1)
                        hi, lo = (w[:, hl, 4 * q:4 * q + 4].rearrange("p j d -> p (j d)") for w in (wvo_hi, wvo_lo))
                        tt(lo, (C.X, C.E)[hl][q][:, :], hi, ALU.subtract).then_inc(wvo_split, 1)

            def q0(a):
                def step(n):
                    dve.wait_ge(a.s_qk, n + 1)
                    for b in range(2):
                        ts(a.q0[:, b], at["hmask"], a.qk[:, 0, S * b:S * b + 1], None, ALU.mult).then_inc(a.s_q0, 1)
                return step

            def v(a):
                def step(n):
                    dve.wait_ge(a.s_qk, n + 1)
                    for b in range(2):
                        tt(a.V[:, b, :, 0:DK0], a.X[:, (2 + b) * P:(3 + b) * P].rearrange("p (h k) -> p h k", k=DK0),
                           at["vmask"].rearrange("p (h k) -> p h k", k=DK0), ALU.mult).then_inc(a.s_v, 1)
                return step

            def nz(a):
                def step(n):
                    dve.wait_ge(a.s_e0, n + 1)
                    ts(a.nz[:], a.E[:, 0:H], 0.0, None, ALU.not_equal).then_inc(a.s_nz, 1)
                return step

            def thr(a, causal):
                def step(n):
                    dve.wait_ge(a.s_cnt, n + 1)
                    if causal:
                        ts(a.thr[:], a.E[:, H:2 * H], at["row1"], None, ALU.min).then_inc(a.s_thr, 1)
                    else:
                        dve.tensor_copy(a.thr[:], a.E[:, H:2 * H]).then_inc(a.s_thr, 1)
                    ts(a.lenpos[:], a.E[:, H:2 * H], 0.0, None, ALU.is_gt).then_inc(a.s_thr, 1)
                    dve.wait_ge(a.s_thr, 2 * n + 1)
                    if first_pair(n):
                        dve.wait_ge(ready, 3)
                    tt(a.mask[:], iota[:], a.thr[:].unsqueeze(1).to_broadcast([P, S, H]),
                       ALU.is_ge).then_inc(a.s_mask, 1)
                return step

            def maximum(a, hf):
                def step(n):
                    dve.wait_ge(a.s_e, 2 * n + 1 + hf)
                    m = a.mx[:, 8 * hf:8 * hf + 8]
                    dve.tensor_reduce(m, heads(a.E[:, :]), AX.X, ALU.max).then_inc(a.s_max, 1)
                return step

            def sub(a, hf):
                def step(n):
                    m = a.mx[:, 8 * hf:8 * hf + 8]
                    dve.wait_ge(a.s_max, 2 * n + 1 + hf)
                    tt(heads(a.S[:, hf * HALF:(hf + 1) * HALF]), heads(a.E[:, :]),
                       m.unsqueeze(2).to_broadcast([P, 8, S]), ALU.subtract).then_inc(a.s_sub, 1)
                return step

            def zn(a):
                def step(n):
                    dve.wait_ge(a.s_z, n + 1)
                    zv = a.X[:, 0:2 * P].rearrange("p (h c) -> p h c", c=SLOT)
                    tt(a.den[:], zv[:, :, DK0], a.lenpos[:], ALU.mult).then_inc(a.s_zn, 1)
                    dve.wait_ge(a.s_zn, 3 * n + 1)
                    dve.reciprocal(a.rd[:], a.den[:]).then_inc(a.s_zn, 1)
                    dve.wait_ge(a.s_zn, 3 * n + 2)
                    tt(a.zn[:].rearrange("p (h k) -> p h k", k=DK0), zv[:, :, 0:DK0],
                       a.rd[:].unsqueeze(2).to_broadcast([P, H, DK0]), ALU.mult).then_inc(a.s_zn, 1)
                return step

            def y(a, l, m, res):
                def step(n):
                    if a is Bc:
                        if reused(n):
                            dve.wait_ge(L3.s_y, n)
                        dve.tensor_copy(m0r[:], x1r[:, D:D + 1]).then_inc(s_m0r, 1)
                    dve.wait_ge(a.s_zn, 3 * n + 3)
                    dve.scalar_tensor_tensor(l.y[:], a.zn[:], m, res, ALU.mult, ALU.add).then_inc(l.s_y, 1)
                return step

            def stats(l):
                def step(n):
                    dve.wait_ge(l.s_y, n + 1)
                    dve.bn_stats(l.st[:], l.y[:]).then_inc(l.s_st, 1)
                    dve.wait_ge(l.s_st, 2 * n + 1)
                    dve.sem_inc(passed, 1)
                    dve.bn_aggr(l.mv[:], l.st[:]).then_inc(l.s_st, 1)
                return step

            def xh(l):
                def step(n):
                    dve.wait_ge(l.s_rstd, 2 * n + 2)
                    ts(l.xh[:], l.y[:], l.mv[:, 0:1], l.rstd[:, 0:1], ALU.subtract, ALU.mult).then_inc(l.s_xh, 1)
                    if l is L1 and first_pair(n):
                        split_folded()
                return step

            def m0(n):
                dve.wait_ge(s_xnl, 16 * n + 16)
                if reused(n):
                    dve.wait_ge(s_h1c, n)
                dve.tensor_reduce(A.am[:], A.xn[:], AX.X, ALU.max, apply_absolute_value=True).then_inc(s_m0, 1)
                dve.wait_ge(s_m0, 2 * n + 1)
                ts(h1[:, D:D + 1], A.am[:], 0.0, None, ALU.is_gt).then_inc(s_m0, 1)

            def b_cm(n):
                dve.wait_ge(s_h1c, n + 1)
                dve.wait_ge(s_cnl, 16 * n + 16)
                dve.tensor_reduce(am1[:], x1r[:, 0:D], AX.X, ALU.max, apply_absolute_value=True).then_inc(s_cm, 1)
                dve.wait_ge(s_cm, 3 * n + 1)
                ts(m1[:], am1[:], 0.0, None, ALU.is_gt).then_inc(s_cm, 1)
                dve.wait_ge(s_cm, 3 * n + 2)
                ts(cm[:], cn[:], m1[:, 0:1], None, ALU.mult).then_inc(s_cm, 1)

            def b_y3(n):
                dve.wait_ge(s_f3, n + 1)
                tt(ffn[:], Bc.E[:, 2 * P:3 * P], vec["fc2_b"], ALU.add).then_inc(s_ffn, 1)
                dve.wait_ge(s_ffn, n + 1)
                dve.wait_ge(s_m0r, n + 1)
                if reused(n):
                    dve.wait_ge(L3.s_xh, n)
                dve.scalar_tensor_tensor(L3.y[:], ffn[:], m0r[:, 0:1], x2[:], ALU.mult, ALU.add
                                         ).then_inc(L3.s_y, 1)

            def ks(g):
                def step(n):
                    if g == 0 and first_pair(n):
                        dve.wait_ge(w_block0, 16 * 10)
                        ts(bq8[:], bq_sb[:], float(DK1) ** -0.5, None, ALU.mult)
                        dve.wait_ge(bvo_ready, 1)
                        tt(obias[:], C.X[1][:, 0:D], vec["bo"], ALU.add).then_inc(bvo_ready, 1)
                    dve.wait_ge(C.s_k, 2 * n + 1 + g)
                    if reused(n):
                        dve.wait_ge(C.s_kz, 32 * n)
                    tt(kst[:, 4 * g:4 * g + 4], C.X[0][:, :].rearrange("p (j t) -> p j t", t=P),
                       bk_sb[:, 4 * g:4 * g + 4].unsqueeze(2).to_broadcast([P, 4, P]), ALU.add).then_inc(C.s_ks, 1)
                return step

            def fadd(g):
                def step(n):
                    dve.wait_ge(C.s_e, 2 * n + 1 + g)
                    if g == 0:
                        dve.wait_ge(C.s_fl, 16 * n + 16)
                    sc = Sc[:, g * HALF:(g + 1) * HALF]
                    dve.scalar_tensor_tensor(sc, f[:].rearrange("p h t -> p (h t)")[:, g * HALF:(g + 1) * HALF], 2.0,
                                             C.E[g][:, :], ALU.mult, ALU.add).then_inc(C.s_s, 1)
                return step

            def c_max(g):
                def step(n):
                    sc = Sc[:, g * HALF:(g + 1) * HALF]
                    dve.wait_ge(C.s_s, 2 * n + 1 + g)
                    dve.tensor_reduce(mxc[:, 8 * g:8 * g + 8], heads(sc), AX.X, ALU.max).then_inc(C.s_max, 1)
                return step

            def den(g):
                def step(n):
                    dve.wait_ge(C.s_p, 2 * n + 1 + g)
                    d = denc[:, 8 * g:8 * g + 8]
                    dve.tensor_reduce(d, heads(Pc[:, g * HALF:(g + 1) * HALF]), AX.X, ALU.add).then_inc(C.s_den, 1)
                    dve.wait_ge(C.s_den, 2 * n + 1 + g)
                    dve.reciprocal(rdc[:, 8 * g:8 * g + 8], d).then_inc(C.s_rd, 1)
                return step

            def nrm(g):
                def step(n):
                    dve.wait_ge(C.s_rd, 2 * n + 1 + g)
                    pr = heads(Pc[:, g * HALF:(g + 1) * HALF])
                    tt(pr, pr, rdc[:, 8 * g:8 * g + 8].unsqueeze(2).to_broadcast([P, 8, S]),
                       ALU.mult).then_inc(C.s_nrm, 1)
                return step

            def c_y(n):
                dve.wait_ge(C.s_o, 2 * n + 2)
                dve.wait_ge(C.s_x3r, n + 1)
                if reused(n):
                    dve.wait_ge(L4.s_xh, n)
                tt(L4.y[:], C.X[1][:, 0:D], x3r[:], ALU.add).then_inc(L4.s_y, 1)

            steps = {"A.m0": m0, "B.cm": b_cm, "B.y3": b_y3, "C.y": c_y,
                     "A.thr": thr(A, True), "B.thr": thr(Bc, False),
                     "A.y": y(A, L1, h1[:, D:D + 1], A.xn[:]), "B.y": y(Bc, L2, m1[:, 0:1], x1r[:, 0:D])}
            for k, l in (("A.", L1), ("B.", L2), ("B.3", L3), ("C.", L4)):
                steps |= {k + "st": stats(l), k + "xh": xh(l)}
            for nm, a in (("A", A), ("B", Bc)):
                steps |= {nm + ".q0": q0(a), nm + ".vz": v(a), nm + ".nz": nz(a), nm + ".zn": zn(a),
                          nm + ".max_0": maximum(a, 0), nm + ".max_1": maximum(a, 1),
                          nm + ".sub_0": sub(a, 0), nm + ".sub_1": sub(a, 1)}
            for g in range(2):
                steps |= {f"C.ks_{g}": ks(g), f"C.fadd_{g}": fadd(g), f"C.max_{g}": c_max(g), f"C.den_{g}": den(g),
                          f"C.nrm_{g}": nrm(g)}
            run(dve, steps, ENG)

        @block.gpsimd
        def _(pool):
            tt, ts = pool.tensor_tensor, pool.tensor_scalar
            pool.memset(Kz[:], 0.0).then_inc(zeroed, 1)

            def kblk(a, hf):
                def step(n):
                    pool.wait_ge(a.s_qk, n + 1)
                    tt(a.kblk[:, 8 * hf:8 * hf + 8], a.qk[:, 1].unsqueeze(1).to_broadcast([P, 8, P]),
                       at["hmask"][:, 8 * hf:8 * hf + 8].unsqueeze(2).to_broadcast([P, 8, P]),
                       ALU.mult).then_inc(a.s_kblk, 1)
                return step

            def rstd(l):
                def step(n):
                    pool.wait_ge(l.s_st, 2 * n + 2)
                    tt(l.ve[:], l.mv[:, 1:2], at[l.eps], ALU.add).then_inc(l.s_rstd, 1)
                    pool.wait_ge(l.s_rstd, 2 * n + 1)
                    tt(l.rstd[:], l.ve[:], at["power"], ALU.pow).then_inc(l.s_rstd, 1)
                return step

            def gb(l, *free):
                def step(n):
                    if first_pair(n):
                        pool.wait_ge(w_block0, 16 * 10)
                    pool.wait_ge(l.s_xh, n + 1)
                    tt(l.xg[:], l.xh[:], l.g, ALU.mult).then_inc(l.s_xg, 1)
                    pool.wait_ge(l.s_xg, n + 1)
                    if reused(n):
                        for readers, per in free:
                            pool.wait_ge(readers, per * n)
                    tt(l.out, l.xg[:], l.b, ALU.add).then_inc(l.s_out, 1)
                return step

            def x3c(n):
                pool.wait_ge(L3.s_out, n + 1)
                if reused(n):
                    pool.wait_ge(L4.s_y, n)
                if first_pair(n):
                    pool.wait_ge(bvo_ready, 2)
                tt(x3r[:], h2[:], obias[:], ALU.add).then_inc(C.s_x3r, 1)

            def clo(n):
                pool.wait_ge(C.s_chi, n + 1)
                tt(cT_lo[:], cT[:], cT_hi[:], ALU.subtract).then_inc(C.s_clo, 1)

            def c_sub(g):
                def step(n):
                    pool.wait_ge(C.s_max, 2 * n + 1 + g)
                    v = heads(Sc[:, g * HALF:(g + 1) * HALF])
                    tt(v, v, mxc[:, 8 * g:8 * g + 8].unsqueeze(2).to_broadcast([P, 8, S]),
                       ALU.subtract).then_inc(C.s_sub, 1)
                return step

            steps = {"C.x3c": x3c, "C.clo": clo, "C.sub_0": c_sub(0), "C.sub_1": c_sub(1),
                     "A.kblk_0": kblk(A, 0), "A.kblk_1": kblk(A, 1), "B.kblk_0": kblk(Bc, 0), "B.kblk_1": kblk(Bc, 1),
                     "A.gb": gb(L1, (s_h1c, 1)),
                     "B.gb": gb(L2, (L3.s_y, 1)),
                     "B.3gb": gb(L3, (C.s_x3r, 1), (C.s_x3t, 1)),
                     "C.gb": gb(L4, (s_st, 16))}
            for k, l in (("A.", L1), ("B.", L2), ("B.3", L3), ("C.", L4)):
                steps[k + "rstd"] = rstd(l)
            pool.wait_ge(w_self, 16 * 4)
            run(pool, steps, ENG)


TURN = """
A.sub_1+3 C.clo+2 C.chi+2 B.e_0+2 C.q_1+1 C.e_0+1 A.pts_0+3 B.pts_1+2 B.e_1+2 A.exp_1+3 C.max_1+1 C.ks_1+2
C.den_0+1 B.pt_0+2 B.zn+2 B.y+2 B.rstd+2 B.st+2 A.e_1+3 C.loadc+2 A.zn+3 C.e_1+1 C.exp_0+1 A.pt_0+3 B.zts+2
A.pts_1+3 B.pt_1+2 A.y+3 B.xh+2 C.k_1+2 C.vz+2 B.pv_0+2 A.st+3 B.pv_1+2 A.pt_1+3 C.nrm_0+1 C.loadf+1
C.exp_1+1 B.gb+2 A.zts+3 C.den_1+1 B.z+2 A.loadx+4 A.xh+3 A.q0+4 C.nrm_1+1 C.st+0 A.nz+4 B.cm+3 C.kz+3
C.vs_0+2 B.y3+2 B.3st+2 A.thr+4 B.3xh+2 A.pv_0+3 A.vz+4 A.rstd+3 A.pv_1+3 C.v_0+2 A.z+3 C.store+0 C.v_1+2
A.qkv+4 B.q0+3 C.v_2+2 B.f1+2 C.pt_0+1 A.gb+3 C.vs_1+2 B.f2+2 A.e0+4 C.xh+0 A.qk+4 B.f1s+2 A.m0+4 B.nz+3
A.kblk_0+4 C.v_3+2 B.f3+2 C.rstd+0 A.max_0+4 C.pt_1+1 B.thr+3 C.o_0+1 C.vs_2+2 A.cnt+4 B.tr+3 C.y+1 C.o_1+1
B.3rstd+2 C.ks_0+3 B.3gb+2 B.f2s+2 B.kblk_0+3 B.qkv+3 B.kblk_1+3 B.max_0+3 B.sub_0+3 C.pts_0+1 A.sub_0+4
B.vz+3 B.h1c+3 C.vs_3+2 A.kblk_1+4 C.fadd_0+2 C.gb+0 A.e_0+4 C.pts_1+1 B.xts+3 C.sub_0+2 B.qk+3 C.x3ts+2
B.max_1+3 B.sub_1+3 B.e0+3 C.x3c+2 C.qs_0+2 B.loadc+4 B.exp_0+3 A.exp_0+4 C.max_0+2 A.max_1+4 C.fadd_1+2
C.qs_1+2 B.pts_0+3 C.sub_1+2 C.x3t+2 C.k_0+3 B.cnt+3 B.exp_1+3 C.q_0+2
"""
ORDER = [(w[0], w[2:].split("+")[0], int(w.split("+")[1])) for w in TURN.split()]
AHEAD = max(k for _, _, k in ORDER)

_OUT = ((B, S, D), "float32")


def kernel(**inputs):
    import concourse.bacc as _bacc
    from concourse.bass_utils import run_bass_kernel_spmd as _run

    g = {k: np.asarray(v) for k, v in inputs.items()}
    L0 = {k[9:]: v for k, v in g.items() if k.startswith("L0_xattn_")}
    L1 = {k[9:]: v for k, v in g.items() if k.startswith("L1_xattn_")}
    T = B * S
    x, c, fs = g["x"], g["ctx_1024"], g["fside_Bx16xSxS2_0"]

    def col(v):
        return v.reshape(J, P).T

    arrays = {
        "consts": constants(),
        "columns": np.repeat(np.arange(S), H)[None].astype(np.float32),
        "x": x.reshape(T, D), "xT": x.reshape(T, D).T, "ctxn": c.reshape(T, D), "ctxT": c.reshape(T, D).T,
        "fs": fs.transpose(0, 2, 1, 3).reshape(T, H * S),
        **{n: L0[n].transpose(1, 0, 2).reshape(D, D) for n in ("Wq1", "Wk1", "Wv1", "Wq2", "Wk2", "Wv2")},
        "fc1T": L0["fc1_w"].T, "fc2T": L0["fc2_w"].T,
        "vecs": np.stack([L0["ln1_g"], L0["ln1_b"], L0["ln2_g"], L0["ln2_b"], L0["ln3_g"], L0["ln3_b"], L1["ln_g"],
                          L1["ln_b"], L1["bo"], L0["fc2_b"]]),
        "fc1b": L0["fc1_b"].reshape(D, 1),
        "wq": L1["wq"], "wk": L1["wk"], "wvT": L1["wv"].T, "wo": L1["wo"],
        "bq": col(L1["bq"]), "bk": col(L1["bk"]), "bv": col(L1["bv"]),
    }
    nc = _bacc.Bacc("TRN2", target_bir_lowering=False, num_devices=1)
    named, args = {}, []
    for name, a in arrays.items():
        a = np.ascontiguousarray(a)
        named[f"in_{name}"] = a
        args.append(nc.dram_tensor(f"in_{name}", a.shape, mybir.dt.from_np(a.dtype), kind="ExternalInput").ap())
    args.append(nc.dram_tensor("out_0", (T, D), F32, kind="ExternalOutput").ap())
    bass_two_blocks(nc, *args)
    r = _run(nc, [named], core_ids=[0])
    return r.results[0]["out_0"].reshape(_OUT[0])
```
